# Optimizing a Trainium2 kernel written in Bass

```python
import numpy as np
import jax
import jax.numpy as jnp

def _softmax(x, axis=-1):
    return jax.nn.softmax(x, axis=axis)

def _gelu(x):
    return jax.nn.gelu(x, approximate=True)

def _silu(x):
    return jax.nn.silu(x)

def _sigmoid(x):
    return jax.nn.sigmoid(x)

def _layernorm(x, axis=-1, eps=1e-05):
    m = jnp.mean(x, axis=axis, keepdims=True)
    v = jnp.var(x, axis=axis, keepdims=True)
    return (x - m) / jnp.sqrt(v + eps)

def _scatter_add(tgt, idx, src, axis=0):
    return tgt.at[idx].add(src)

def _segment_sum(src, seg, n):
    return jax.ops.segment_sum(src, seg, n)
kernel_name = 'mk_prb_d2_jaxref_r4_4f7185'

def setup_inputs(seed: int=0):
    np.random.seed(seed)
    _w = jnp.asarray

    def _L0_attn_setup():
        import jax, jax.numpy as jnp
        import numpy as np
        from jax import lax
        B, T, HID, H, DK, DV, K = (2, 512, 256, 16, 64, 64, 4)
        SCALE = float(DK) ** (-0.5)
        EPS = 1e-05

        def _causal_dwconv_silu(z, w, b):
            zc = z.transpose(0, 2, 1)
            y = lax.conv_general_dilated(zc, w, (1,), [(K - 1, 0)], dimension_numbers=('NCH', 'OIH', 'NCH'), feature_group_count=zc.shape[1])
            return jax.nn.silu((y + b[None, :, None]).transpose(0, 2, 1))
        key = jax.random.key(seed)
        ks = jax.random.split(key, 12)
        n = lambda k, sh, s=0.02: jax.random.normal(k, sh, jnp.float32) * s
        return {'x': jax.random.normal(ks[0], (B, T, HID), jnp.float32), 'Wq': n(ks[1], (H * DK, HID)), 'Wk': n(ks[2], (H * DK, HID)), 'Wv': n(ks[3], (H * DV, HID)), 'Wa': n(ks[4], (H * DV, HID)), 'ba': jnp.zeros((H * DV,), jnp.float32), 'Wb': n(ks[5], (H, HID)), 'bb': jnp.zeros((H,), jnp.float32), 'Wg': n(ks[6], (H * DV, HID)), 'Wo': n(ks[7], (HID, H * DV)), 'qcw': n(ks[8], (H * DK, 1, K), 0.3), 'qcb': jnp.zeros((H * DK,), jnp.float32), 'kcw': n(ks[9], (H * DK, 1, K), 0.3), 'kcb': jnp.zeros((H * DK,), jnp.float32), 'vcw': n(ks[10], (H * DV, 1, K), 0.3), 'vcb': jnp.zeros((H * DV,), jnp.float32), 'ln_w': jnp.ones((DV,), jnp.float32), 'ln_b': jnp.zeros((DV,), jnp.float32)}
    _L0_attn_in = _L0_attn_setup()

    def _L0_ffn_setup():
        import jax, jax.numpy as jnp
        import numpy as np
        B, S, D, E, R, TOP_K = (4, 1024, 256, 10, 4, 2)
        SCALING = 1.0 / R
        key = jax.random.key(seed)
        ks = jax.random.split(key, 7)
        return {'x': jax.random.normal(ks[0], (B, S, D), dtype=jnp.float32), 'W_base': jax.random.normal(ks[1], (D, D), dtype=jnp.float32) * D ** (-0.5), 'b_base': jax.random.normal(ks[2], (D,), dtype=jnp.float32) * 0.02, 'gate_W': jax.random.normal(ks[3], (E, D), dtype=jnp.float32) * D ** (-0.5), 'gate_b': jax.random.normal(ks[4], (E,), dtype=jnp.float32) * 0.02, 'lora_down': jax.random.normal(ks[5], (E, R, D), dtype=jnp.float32) * D ** (-0.5), 'lora_up': jax.random.normal(ks[6], (E, D, R), dtype=jnp.float32) * R ** (-0.5)}
    _L0_ffn_in = _L0_ffn_setup()

    def _L1_attn_setup():
        import jax, jax.numpy as jnp
        import numpy as np
        B, S, C = (4, 512, 256)
        E, H = (256, 16)
        D = E // H
        key = jax.random.key(seed)
        k1, k2, k3, k4, k5 = jax.random.split(key, 5)
        s = 1.0 / np.sqrt(C)
        return {'x': jax.random.normal(k1, (B, S, C), dtype=jnp.float32), 'w_qkv': jax.random.uniform(k2, (C, 3 * E), minval=-s, maxval=s, dtype=jnp.float32), 'b_qkv': jax.random.uniform(k3, (3 * E,), minval=-s, maxval=s, dtype=jnp.float32), 'w_out': jax.random.uniform(k4, (E, E), minval=-1.0 / np.sqrt(E), maxval=1.0 / np.sqrt(E), dtype=jnp.float32), 'b_out': jax.random.uniform(k5, (E,), minval=-1.0 / np.sqrt(E), maxval=1.0 / np.sqrt(E), dtype=jnp.float32)}
    _L1_attn_in = _L1_attn_setup()

    def _L1_ffn_setup():
        import jax, jax.numpy as jnp
        import numpy as np
        INT4_QMAX = 7.0

        def simulate_quantize_int4(w):
            scale = jnp.max(jnp.abs(w)) / INT4_QMAX
            q = jnp.clip(jnp.round(w / scale), -8.0, 7.0)
            return q * scale
        key = jax.random.key(seed)
        k_x, k_w, k_bias, k_a, k_b = jax.random.split(key, 5)
        d_in, features, rank = (256, 256, 16)
        x = jax.random.normal(k_x, (4, 2048, d_in), dtype=jnp.float32)
        kernel = jax.random.normal(k_w, (d_in, features), dtype=jnp.float32)
        bias = jax.random.normal(k_bias, (features,), dtype=jnp.float32)
        a = jax.random.normal(k_a, (d_in, rank), dtype=jnp.float32) * (1.0 / np.sqrt(d_in))
        b = jax.random.normal(k_b, (rank, features), dtype=jnp.float32) * 0.01
        return {'x': x, 'kernel': kernel, 'bias': bias, 'a': a, 'b': b}
    _L1_ffn_in = _L1_ffn_setup()
    _d = {'L0_attn_x': _L0_attn_in['x'], 'L0_attn_Wq': _L0_attn_in['Wq'], 'L0_attn_Wk': _L0_attn_in['Wk'], 'L0_attn_Wv': _L0_attn_in['Wv'], 'L0_attn_Wa': _L0_attn_in['Wa'], 'L0_attn_ba': _L0_attn_in['ba'], 'L0_attn_Wb': _L0_attn_in['Wb'], 'L0_attn_bb': _L0_attn_in['bb'], 'L0_attn_Wg': _L0_attn_in['Wg'], 'L0_attn_Wo': _L0_attn_in['Wo'], 'L0_attn_qcw': _L0_attn_in['qcw'], 'L0_attn_qcb': _L0_attn_in['qcb'], 'L0_attn_kcw': _L0_attn_in['kcw'], 'L0_attn_kcb': _L0_attn_in['kcb'], 'L0_attn_vcw': _L0_attn_in['vcw'], 'L0_attn_vcb': _L0_attn_in['vcb'], 'L0_attn_ln_w': _L0_attn_in['ln_w'], 'L0_attn_ln_b': _L0_attn_in['ln_b'], 'L0_ffn_W_base': _L0_ffn_in['W_base'], 'L0_ffn_b_base': _L0_ffn_in['b_base'], 'L0_ffn_gate_W': _L0_ffn_in['gate_W'], 'L0_ffn_gate_b': _L0_ffn_in['gate_b'], 'L0_ffn_lora_down': _L0_ffn_in['lora_down'], 'L0_ffn_lora_up': _L0_ffn_in['lora_up'], 'L1_attn_w_qkv': _L1_attn_in['w_qkv'], 'L1_attn_b_qkv': _L1_attn_in['b_qkv'], 'L1_attn_w_out': _L1_attn_in['w_out'], 'L1_attn_b_out': _L1_attn_in['b_out'], 'L1_ffn_kernel': _L1_ffn_in['kernel'], 'L1_ffn_bias': _L1_ffn_in['bias'], 'L1_ffn_a': _L1_ffn_in['a'], 'L1_ffn_b': _L1_ffn_in['b']}
    _x0 = _d['L0_attn_x']
    _d['L0_attn_x'] = jax.random.normal(jax.random.fold_in(jax.random.key(seed), 1), (16, 512, 256), dtype=_x0.dtype)
    del _x0
    return _d

def reference(L0_attn_x, L0_attn_Wq, L0_attn_Wk, L0_attn_Wv, L0_attn_Wa, L0_attn_ba, L0_attn_Wb, L0_attn_bb, L0_attn_Wg, L0_attn_Wo, L0_attn_qcw, L0_attn_qcb, L0_attn_kcw, L0_attn_kcb, L0_attn_vcw, L0_attn_vcb, L0_attn_ln_w, L0_attn_ln_b, L0_ffn_W_base, L0_ffn_b_base, L0_ffn_gate_W, L0_ffn_gate_b, L0_ffn_lora_down, L0_ffn_lora_up, L1_attn_w_qkv, L1_attn_b_qkv, L1_attn_w_out, L1_attn_b_out, L1_ffn_kernel, L1_ffn_bias, L1_ffn_a, L1_ffn_b):

    def _L0_attn_ref(x, Wq, Wk, Wv, Wa, ba, Wb, bb, Wg, Wo, qcw, qcb, kcw, kcb, vcw, vcb, ln_w, ln_b):
        import jax, jax.numpy as jnp
        import numpy as np
        from jax import lax
        B, T, HID, H, DK, DV, K = (2, 512, 256, 16, 64, 64, 4)
        SCALE = float(DK) ** (-0.5)
        EPS = 1e-05

        def _causal_dwconv_silu(z, w, b):
            zc = z.transpose(0, 2, 1)
            y = lax.conv_general_dilated(zc, w, (1,), [(K - 1, 0)], dimension_numbers=('NCH', 'OIH', 'NCH'), feature_group_count=zc.shape[1])
            return jax.nn.silu((y + b[None, :, None]).transpose(0, 2, 1))
        Bb, Tt, _ = x.shape
        q = _causal_dwconv_silu(x @ Wq.T, qcw, qcb).reshape(Bb, Tt, H, DK)
        k = _causal_dwconv_silu(x @ Wk.T, kcw, kcb).reshape(Bb, Tt, H, DK) * SCALE
        v = _causal_dwconv_silu(x @ Wv.T, vcw, vcb).reshape(Bb, Tt, H, DV)
        a = jax.nn.sigmoid(x @ Wa.T + ba).reshape(Bb, Tt, H, DV)
        beta = jax.nn.sigmoid(x @ Wb.T + bb)

        def step(S, inp):
            qt, kt, vt, at, bt = inp
            err = jnp.einsum('bhij,bhj->bhi', S, kt) - vt
            S = at[..., None] * S - bt[..., None, None] * (err[..., None] * kt[:, :, None, :])
            o = jnp.einsum('bhij,bhj->bhi', S, qt)
            return (S, o)
        xs = tuple((jnp.moveaxis(t, 1, 0) for t in (q, k, v, a, beta)))
        S0 = jnp.zeros((Bb, H, DV, DK), x.dtype)
        _, o = lax.scan(step, S0, xs)
        o = jnp.moveaxis(o, 0, 1)
        mu = o.mean(-1, keepdims=True)
        var = ((o - mu) ** 2).mean(-1, keepdims=True)
        o = (o - mu) / jnp.sqrt(var + EPS) * ln_w + ln_b
        g = jax.nn.sigmoid(x @ Wg.T).reshape(Bb, Tt, H, DV)
        o = (o * g).reshape(Bb, Tt, H * DV)
        return o @ Wo.T

    def _L0_ffn_ref(x, W_base, b_base, gate_W, gate_b, lora_down, lora_up):
        import jax, jax.numpy as jnp
        import numpy as np
        B, S, D, E, R, TOP_K = (4, 1024, 256, 10, 4, 2)
        SCALING = 1.0 / R
        base_out = jnp.einsum('bsd,od->bso', x, W_base) + b_base
        logits = jnp.einsum('bsd,ed->bse', x, gate_W) + gate_b
        top_vals, top_idx = jax.lax.top_k(logits, TOP_K)
        top_w = jax.nn.softmax(top_vals, axis=-1)
        weights = jnp.sum(top_w[..., None] * jax.nn.one_hot(top_idx, E, dtype=x.dtype), axis=-2)
        h = jnp.einsum('bsd,erd->bser', x, lora_down)
        h = h * weights[..., None]
        lora_out = jnp.einsum('bser,edr->bsd', h, lora_up) * SCALING
        return base_out + lora_out

    def _L1_attn_ref(x, w_qkv, b_qkv, w_out, b_out):
        import jax, jax.numpy as jnp
        import numpy as np
        B, S, C = (4, 512, 256)
        E, H = (256, 16)
        D = E // H
        b, s, _ = x.shape
        qkv = x @ w_qkv + b_qkv
        qkv = qkv.reshape(b, s, 3, H, D)
        q = qkv[:, :, 0].transpose(0, 2, 1, 3)
        k = qkv[:, :, 1].transpose(0, 2, 1, 3)
        v = qkv[:, :, 2].transpose(0, 2, 1, 3)
        scale = jnp.asarray(D, x.dtype) ** 0.5
        scores = jnp.einsum('bhqd,bhkd->bhqk', q, k) / scale
        attn = jax.nn.softmax(scores, axis=-1)
        out = jnp.einsum('bhqk,bhkd->bhqd', attn, v)
        out = out.transpose(0, 2, 1, 3).reshape(b, s, E)
        return out @ w_out + b_out

    def _L1_ffn_ref(x, kernel, bias, a, b):
        import jax, jax.numpy as jnp
        import numpy as np
        INT4_QMAX = 7.0

        def simulate_quantize_int4(w):
            scale = jnp.max(jnp.abs(w)) / INT4_QMAX
            q = jnp.clip(jnp.round(w / scale), -8.0, 7.0)
            return q * scale
        w = simulate_quantize_int4(kernel)
        y = jnp.einsum('bsd,df->bsf', x, w) + bias
        lora = jnp.einsum('bsr,rf->bsf', jnp.einsum('bsd,dr->bsr', x, a), b)
        return y + lora
    x = L0_attn_x
    xn = _layernorm(x, axis=-1)
    x = x + _L0_attn_ref(xn, L0_attn_Wq, L0_attn_Wk, L0_attn_Wv, L0_attn_Wa, L0_attn_ba, L0_attn_Wb, L0_attn_bb, L0_attn_Wg, L0_attn_Wo, L0_attn_qcw, L0_attn_qcb, L0_attn_kcw, L0_attn_kcb, L0_attn_vcw, L0_attn_vcb, L0_attn_ln_w, L0_attn_ln_b) + _L0_ffn_ref(xn, L0_ffn_W_base, L0_ffn_b_base, L0_ffn_gate_W, L0_ffn_gate_b, L0_ffn_lora_down, L0_ffn_lora_up)
    xn = _layernorm(x, axis=-1)
    x = x + _L1_attn_ref(xn, L1_attn_w_qkv, L1_attn_b_qkv, L1_attn_w_out, L1_attn_b_out) + _L1_ffn_ref(xn, L1_ffn_kernel, L1_ffn_bias, L1_ffn_a, L1_ffn_b)
    return x

_drawn_inputs = setup_inputs


def setup_inputs(seed=0):
    import zlib

    import numpy as np

    out = dict(_drawn_inputs(seed))
    spreads = {'L0_attn_ba': (0.0, 0.8),
     'L0_attn_bb': (0.0, 0.8),
     'L0_attn_qcb': (0.0, 0.373),
     'L0_attn_kcb': (0.0, 0.308),
     'L0_attn_vcb': (0.0, 0.304),
     'L0_attn_ln_w': (1.0, 0.6),
     'L0_attn_ln_b': (0.0, 0.376)}
    factors = {'L0_attn_Wa': 8.0,
     'L0_attn_Wb': 8.0,
     'L0_attn_Wg': 7.266,
     'L0_ffn_b_base': 4.873,
     'L0_ffn_gate_b': 4.966,
     'L1_attn_w_qkv': 8.0,
     'L1_attn_b_qkv': 8.0,
     'L1_attn_w_out': 8.0,
     'L1_attn_b_out': 45.068,
     'L1_ffn_a': 8.0,
     'L1_ffn_b': 8.0}
    for name, (base, spread) in spreads.items():
        noise = np.random.default_rng([zlib.crc32(name.encode()), seed]).standard_normal(out[name].shape)
        drawn = base * np.exp(spread * noise) if base else spread * noise
        out[name] = jnp.asarray(drawn.astype(out[name].dtype))
    for name, factor in factors.items():
        out[name] = (out[name] * factor).astype(out[name].dtype)
    return out
```

```python
import numpy as np
import concourse.bass as bass
from concourse import mybir
from contextlib import ExitStack

B, T, HID = 16, 512, 256
H, DK, DV, TAPS = 16, 64, 64, 4
HD = H * DV
C = 16
GB = 8
GROUPS = B // GB
P = GB * C
STEPS = (T // C) * GROUPS
HP = H // 2
NQ = GB // 2
MT = 3 * HD // 128
ROW = DV + C
SLOT = DV + 2 * C
E, R = 10, 4
ER = E * R
EPS = 1e-5
F1_USES, F2_USES = 10, 4
F_USES = F1_USES + F2_USES
F_BANKS = 2
CONV_OPS = MT * (TAPS - 1)
SOLVE_OPS = 2 + C + 3 * (C - 1) + 1
DECAY_OPS = C
POOL_OPS = DECAY_OPS + 2 + 3 * C
RSQRT_OPS = 14

H1, D1 = 16, 16
NT = T // 128
HG = H1 // 4
RSQRT_MAGIC = float(0x5F3759DF)
ROUND = 1.5 * 2.0 ** 23

f32 = mybir.dt.float32
i32 = mybir.dt.int32
u32 = mybir.dt.uint32
ALU = mybir.AluOpType
ACT = mybir.ActivationFunctionType
AX = mybir.AxisListType


def due(value):
    return not isinstance(value, int) or value > 0


def held(engine, passed):
    engine.sem_inc(passed, 1)


def rsqrt_ops(nc, y, v, t, link):
    link(nc.vector.tensor_scalar(t.bitcast(i32), v.bitcast(i32), 1, None, ALU.logical_shift_right))
    link(nc.vector.tensor_scalar(y.bitcast(i32), t.bitcast(i32), -1.0, RSQRT_MAGIC, ALU.mult, ALU.add))
    for _ in range(3):
        link(nc.vector.tensor_tensor(t, y, y, ALU.mult))
        link(nc.vector.tensor_tensor(t, t, v, ALU.mult))
        link(nc.vector.tensor_scalar(t, t, -0.5, 1.5, ALU.mult, ALU.add))
        link(nc.vector.tensor_tensor(y, y, t, ALU.mult))


def dma_of(sems, n, g, ahead, each=16):
    return sems[(g + ahead) % GROUPS], each * (n + (g + ahead) // GROUPS + 1)


def slot_loop(engine, slot, first, last, loop):
    for s in range(first, loop[0]):
        slot(s, (s - s % 2) // 2, s % 2, s, s)
    with engine.Fori(0, (loop[1] - loop[0] + 1) // 2) as i:
        for g in range(2):
            slot(2 * i + (loop[0] + g), i + loop[0] // 2, g, loop[0], loop[1])
    for s in range(loop[1] + 1, last + 1):
        slot(s, (s - s % 2) // 2, s % 2, s, s)


def layer0_recurrence(nc, ins, o_dram):
    def dram(name, shape):
        return nc.dram_tensor(name, shape, f32).ap()

    prod_dram = [dram(f"prod_dram{g}", [GB * 4, P, ROW]) for g in range(GROUPS)]
    v_dram = [dram(f"v_dram{g}", [C, GB, H, DV]) for g in range(GROUPS)]
    a_dram = [dram(f"a_dram{g}", [C, GB, H, DV]) for g in range(GROUPS)]
    beta_dram = [dram(f"beta_dram{g}", [GB, H, C]) for g in range(GROUPS)]
    upd_dram = [dram(f"upd_dram{g}", [GB, H, C, DV]) for g in range(GROUPS)]
    decay_dram = [dram(f"decay_dram{g}", [GB * H, DV]) for g in range(GROUPS)]
    x = ins["L0_attn_x"]

    with ExitStack() as ctx:
        def sb(name, shape, dt=f32):
            return ctx.enter_context(nc.sbuf_tensor(name, shape, dt))

        def ps(name, shape):
            return ctx.enter_context(nc.psum_tensor(name, shape, f32))

        def sem(name):
            return ctx.enter_context(nc.semaphore(name))

        ident = sb("ident", [128, 128])
        ones = sb("ones", [1, 128])
        wqkv = sb("wqkv", [128, 2, 3 * HD])
        wa = sb("wa", [128, 2, HD])
        wbeta = sb("wbeta", [128, 2, H])
        ba = sb("ba", [1, HD])
        bb = sb("bb", [H, 1])
        conv_w = sb("conv_w", [128, MT, TAPS])
        conv_b = sb("conv_b", [128, MT])
        xt = sb("xt", [P, 2, HID])
        xn = sb("xn", [P, HID])
        xnT = sb("xnT", [128, 2, 2, P])
        y = sb("y", [128, MT, GB, TAPS - 1 + C])
        halo = sb("halo", [128, 2, MT, GB, TAPS - 1])
        z = sb("z", [128, MT, P])
        sg = sb("sg", [128, 2, HP, P])
        bt = sb("bt", [H, 2, P])
        vt, at = (sg[:, i].rearrange("p h t -> p (h t)") for i in range(2))
        st = [sb(f"st{g}", [128, GB, HP, SLOT]) for g in range(GROUPS)]
        decay_or_prod = sb("decay_or_prod", [128, GB * HP * DV])
        db = decay_or_prod[:].rearrange("p (m i) -> p m i", i=DV)
        prod = decay_or_prod[:, 0:GB * 4 * ROW].rearrange("p (b c) -> p b c", b=GB)
        kp = sb("kp", [128, C, ROW])
        qp = sb("qp", [128, 2, C, ROW])
        vb = sb("vb", [128, 2, C, DV])
        ab = sb("ab", [128, 2, C, DV])
        nb = sb("nb", [128, 2, C])
        eb = sb("eb", [128, C, DV])
        acb = sb("acb", [128, DV])
        t2 = sb("t2", [128, C - 1, DV])
        pt2 = sb("pt2", [128, C, DV])
        kt = sb("kt", [P, 2, HD])
        xd = sb("xd", [P, H, 2, DV])
        bst = sb("bst", [P, 6])
        mv = sb("mv", [P, 2])
        var = sb("var", [P, 1])
        rs = sb("rs", [P, 1])
        rstmp = sb("rstmp", [P, 1])

        p_bank = [ps(f"p_bank{i}", [128, 512]) for i in range(2)]
        f_bank = [ps(f"f_bank{i}", [128, 512]) for i in range(F_BANKS)]
        d_bank = [ps(f"d_bank{i}", [128, 512]) for i in range(2)]

        consts_in = sem("consts_in")
        ident_done = sem("ident_done")
        init_done = sem("init_done")
        x_in = [sem(f"x_in{g}") for g in range(GROUPS)]
        xn_ready, norm_chain = sem("xn_ready"), sem("norm_chain")
        f_filled, f_freed = sem("f_filled"), sem("f_freed")
        p_filled, p_freed = sem("p_filled"), sem("p_freed")
        d_filled, d_freed = sem("d_filled"), sem("d_freed")
        keys_placed = sem("keys_placed")
        conv_chain, sg_ready, silu_done = sem("conv_chain"), sem("sg_ready"), sem("silu_done")
        halo_done, bneg_done = sem("halo_done"), sem("bneg_done")
        a_wr, beta_wr, v_wr, p_wr, qp_in, kp_in, vb_in, ab_in, nb_in, upd_wr, xd_in, dec_wr, db_in, o_wr = (
            [sem(f"{name}{g}") for g in range(GROUPS)] for name in
            ("a_wr", "beta_wr", "v_wr", "p_wr", "qp_in", "kp_in", "vb_in", "ab_in", "nb_in", "upd_wr", "xd_in",
             "dec_wr", "db_in", "o_wr"))
        solve_chain, pool_chain = sem("solve_chain"), sem("pool_chain")
        decayed = sem("decayed")
        sp_passed, pool_passed, pe_passed, dve_passed = map(sem, ("sp_passed", "pool_passed", "pe_passed", "dve_passed"))

        FIRST, LOOP, LAST = -2, (4, STEPS - 5), STEPS
        block = ctx.enter_context(nc.Block())

        def valid(lo, hi):
            return 0 <= lo and hi < STEPS

        def updates(lo, hi):
            return 0 <= lo and hi < STEPS - GROUPS

        @block.sync
        def _(sp):
            for tile, src in (
                (wqkv[:], ins["wqkv"].rearrange("(k p) n -> p k n", p=128)),
                (wa[:], ins["wa"].rearrange("(k p) n -> p k n", p=128)),
                (wbeta[:], ins["wbeta"].rearrange("(k p) n -> p k n", p=128)),
                (ba[:], ins["L0_attn_ba"].rearrange("(a n) -> a n", a=1)),
                (bb[:], ins["L0_attn_bb"].rearrange("(n a) -> n a", a=1)),
                (conv_w[:], ins["conv_w"]),
                (conv_b[:], ins["conv_b"]),
            ):
                sp.dma_start(tile, src).then_inc(consts_in, 16)

            def load_x(n, g):
                src = x[GB * g:GB * g + GB].rearrange("b (n t) c -> n b t c", t=C)
                sp.dma_start(xt[:, g, :], src[bass.ds(n, 1)]).then_inc(x_in[g], 16)

            load_x(0, 0)

            def slot(s, n, g, lo, hi):
                o = 1 - g
                if updates(lo - 1, hi - 1):
                    t = s - 1
                    sp.wait_ge(pool_chain, POOL_OPS * t + DECAY_OPS)
                    held(sp, sp_passed)
                    if due(dma_of(db_in, n, g, -3, 32)[1]):
                        sp.wait_ge(*dma_of(db_in, n, g, -3, 32))
                        held(sp, sp_passed)
                    sp.dma_start(decay_dram[o], acb[:]).then_inc(dec_wr[o], 16)
                    sp.wait_ge(*dma_of(dec_wr, n, g, -1))
                    held(sp, sp_passed)
                    sp.wait_ge(*dma_of(p_wr, n, g, 0))
                    held(sp, sp_passed)
                    for par in range(2):
                        src = decay_dram[o].rearrange("(m two) i -> two m i", two=2)[par:par + 1]
                        sp.dma_start(db[64 * par:64 * par + 64], src.to_broadcast([64, GB * HP, DV])).then_inc(db_in[o], 16)
                    sp.wait_ge(solve_chain, SOLVE_OPS * (t + 1))
                    held(sp, sp_passed)
                    if due(dma_of(xd_in, n, g, -3, 16 * GB)[1]):
                        sp.wait_ge(*dma_of(xd_in, n, g, -3, 16 * GB))
                        held(sp, sp_passed)
                    sp.dma_start(upd_dram[o].rearrange("b h t i -> (b h) (t i)"), eb[:]).then_inc(upd_wr[o], 16)
                    sp.wait_ge(*dma_of(upd_wr, n, g, -1))
                    held(sp, sp_passed)
                    if due(8 * t):
                        sp.wait_ge(d_filled, 8 * t)
                        held(sp, sp_passed)
                    for b in range(GB):
                        sp.dma_start(xd[C * b:C * b + C, :, b % 2, :],
                                     upd_dram[o][b].rearrange("h t i -> t h i")).then_inc(xd_in[o], 16)
                if valid(lo - 1, hi - 1):
                    t = s - 1
                    sp.wait_ge(pool_chain, POOL_OPS * (t + 1))
                    held(sp, sp_passed)
                    dst = o_dram.rearrange("(n t) b h i -> n t b h i", t=C)[:, :, GB * o:GB * o + GB]
                    sp.dma_start(dst[bass.ds(n - 1 + g, 1)].rearrange("o t b h i -> (o b h) t i"), qp[:, o, :, 0:DV]).then_inc(o_wr[o], 16)
                if valid(lo + 1, hi + 1):
                    t = s + 1
                    if due(POOL_OPS * (t - 1)):
                        sp.wait_ge(pool_chain, POOL_OPS * (t - 1))
                        held(sp, sp_passed)
                    sp.wait_ge(*dma_of(v_wr, n, g, 1))
                    held(sp, sp_passed)
                    sp.dma_start(vb[:, o], v_dram[o].rearrange("t b h i -> (b h) t i")).then_inc(vb_in[o], 16)
                    sp.wait_ge(*dma_of(a_wr, n, g, 1))
                    held(sp, sp_passed)
                    sp.dma_start(ab[:, o], a_dram[o].rearrange("t b h i -> (b h) t i")).then_inc(ab_in[o], 16)
                    sp.wait_ge(*dma_of(beta_wr, n, g, 1))
                    held(sp, sp_passed)
                    sp.dma_start(nb[:, o], beta_dram[o].rearrange("b h t -> (b h) t")).then_inc(nb_in[o], 16)
                    sp.wait_ge(*dma_of(p_wr, n, g, 1))
                    held(sp, sp_passed)
                    if due(dma_of(o_wr, n, g, -1)[1]):
                        sp.wait_ge(*dma_of(o_wr, n, g, -1))
                        held(sp, sp_passed)
                    src = prod_dram[o].rearrange("m (h k r) c -> (m h) k r c", h=4, k=2)
                    sp.dma_start(qp[:, o], src[:, 1]).then_inc(qp_in[o], 16)
                    if due(SOLVE_OPS * t):
                        sp.wait_ge(solve_chain, SOLVE_OPS * t)
                        held(sp, sp_passed)
                    sp.dma_start(kp[:], src[:, 0]).then_inc(kp_in[o], 16)
                if valid(lo + 3, hi + 3):
                    t = s + 3
                    if due(t - 1):
                        sp.wait_ge(xn_ready, t - 1)
                        held(sp, sp_passed)
                    load_x(n + 1 + g, o)
                if lo == LAST:
                    for g in range(GROUPS):
                        sp.wait_ge(o_wr[g], 16 * STEPS // GROUPS)

            slot_loop(sp, slot, FIRST, LAST, LOOP)

        @block.gpsimd
        def _(pool):
            nc.gpsimd.memset(ident[:], 0.0).then_inc(ident_done, 1)
            pool.wait_ge(ident_done, 1)
            nc.gpsimd.affine_select(out=ident[:], in_=ident[:], compare_op=ALU.not_equal, fill=1.0, base=0,
                                    pattern=[[-1, 128]], channel_multiplier=1).then_inc(ident_done, 1)
            pool.wait_ge(init_done, 1)

            def slot(s, n, g, lo, hi):
                if not valid(lo, hi):
                    return
                base, made = POOL_OPS * s, [0]

                def link(ins, back=0):
                    made[0] += 1
                    ins.then_inc(pool_chain, 1)
                    pool.wait_ge(pool_chain, base + made[0])

                pool.wait_ge(*dma_of(ab_in, n, g, 0))
                pool.wait_ge(*dma_of(nb_in, n, g, 0))
                if updates(lo - 1, hi - 1):
                    pool.wait_ge(*dma_of(upd_wr, n, g, -1))
                if due(SOLVE_OPS * s):
                    pool.wait_ge(solve_chain, SOLVE_OPS * s)
                held(pool, pool_passed)
                link(nc.gpsimd.tensor_copy(eb[:, C - 2, :], ab[:, g, C - 1, :]))
                for r in range(C - 3, -1, -1):
                    link(nc.gpsimd.tensor_tensor(eb[:, r, :], eb[:, r + 1, :], ab[:, g, r + 1, :], ALU.mult))
                if updates(lo - 1, hi - 1):
                    pool.wait_ge(*dma_of(dec_wr, n, g, -1))
                link(nc.gpsimd.tensor_tensor(acb[:], eb[:, 0, :], ab[:, g, 0, :], ALU.mult))
                link(nc.gpsimd.tensor_tensor(eb[:, 0:C - 1], eb[:, 0:C - 1],
                                             nb[:, g, 0:C - 1].unsqueeze(2).to_broadcast([128, C - 1, DV]), ALU.mult))
                held(pool, pool_passed)
                link(nc.gpsimd.tensor_copy(eb[:, C - 1, :], nb[:, g, C - 1:C].to_broadcast([128, DV])))
                for r in range(C):
                    q = qp[:, g, r:C, 0:DV]
                    w = C - r
                    pool.wait_ge(solve_chain, SOLVE_OPS * s + 2 + 4 * r + 1)
                    link(nc.gpsimd.tensor_tensor(q, q, ab[:, g, r:r + 1, :].to_broadcast([128, w, DV]), ALU.mult))
                    link(nc.gpsimd.tensor_tensor(
                        pt2[:, 0:w], qp[:, g, r:C, DV + r:DV + r + 1].to_broadcast([128, w, DV]),
                        vb[:, g, r:r + 1, :].to_broadcast([128, w, DV]), ALU.mult))
                    link(nc.gpsimd.tensor_tensor(q, q, pt2[:, 0:w], ALU.add))
                assert made[0] == POOL_OPS

            slot_loop(pool, slot, FIRST, LAST, LOOP)

        @block.tensor
        def _(pe):
            pe.wait_ge(consts_in, 16 * 7)
            pe.wait_ge(ident_done, 2)
            pe.wait_ge(init_done, 1)

            def use(s, k):
                if due(F_USES * s + k - F_BANKS + 1):
                    pe.wait_ge(f_freed, F_USES * s + k - F_BANKS + 1)
                return f_bank[k % F_BANKS]

            def update(s, n, g):
                pe.wait_ge(f_freed, F_USES * s + F1_USES + 2)
                pe.wait_ge(*dma_of(xd_in, n, g, 0, 16 * GB))
                for u in range(8):
                    q, hh = u // 2, u % 2
                    if due(8 * s + u - 1):
                        pe.wait_ge(d_freed, 8 * s + u - 1)
                    for k in range(4):
                        for par in range(2):
                            h = 2 * (4 * hh + k) + par
                            mm = nc.tensor.matmul(d_bank[u % 2][64 * par:64 * par + 64, 128 * k:128 * k + 128],
                                                  kt[32 * q:32 * q + 32, g, DK * h:DK * h + DK],
                                                  xd[32 * q:32 * q + 32, h, :, :], start=True, stop=True)
                    mm.then_inc(d_filled, 1)

            def front2(s, n, g):
                for j in range(4):
                    bank = use(s, F1_USES + j)
                    pe.wait_ge(silu_done, 3 * s + 2 + j // 2)
                    for i in range(4):
                        mm = nc.tensor.transpose(bank[:, 128 * i:128 * i + 128], z[:, HP + 4 * j + i, :], ident[:])
                    mm.then_inc(f_filled, 1)

            def products(s, n, g):
                if due(8 * (s - 1)):
                    pe.wait_ge(d_freed, 8 * (s - 1))
                pe.wait_ge(silu_done, 3 * s + 1)
                pe.wait_ge(keys_placed, s + 1)
                for b in range(GB):
                    if due(8 * s + b - 1):
                        pe.wait_ge(p_freed, 8 * s + b - 1)
                    held(pe, pe_passed)
                    for hq in range(4):
                        for hpo in range(2):
                            for par in range(2):
                                at_ = 32 * (2 * hpo + par)
                                slot_ = st[g][64 * par:64 * par + 64, b, 2 * hq + hpo, :]
                                mm = nc.tensor.matmul(p_bank[b % 2][at_:at_ + 32, ROW * hq:ROW * hq + ROW],
                                                      slot_[:, DV:DV + 2 * C], slot_[:, 0:ROW], start=True, stop=True)
                    mm.then_inc(p_filled, 1)

            def front1(s, n, g):
                bank = use(s, 0)
                pe.wait_ge(xn_ready, s + 1)
                for k in range(2):
                    mm = nc.tensor.transpose(bank[:, 128 * k:128 * k + 128], xn[:, 128 * k:128 * k + 128], ident[:])
                mm.then_inc(f_filled, 1)
                pe.wait_ge(f_freed, F_USES * s + 1)
                for j in range(6):
                    bank = use(s, 1 + j)
                    for i in range(4):
                        m = 4 * j + i
                        for k in range(2):
                            mm = nc.tensor.matmul(bank[:, 128 * i:128 * i + 128], wqkv[:, k, 128 * m:128 * m + 128],
                                                  xnT[:, g, k, :], start=k == 0, stop=k == 1)
                    mm.then_inc(f_filled, 1)
                for j in range(2):
                    bank = use(s, 7 + j)
                    for k in range(2):
                        nc.tensor.matmul(bank[:], xnT[:, g, k, :], wa[:, k, 512 * j:512 * j + 512], start=k == 0, stop=False)
                    nc.tensor.matmul(bank[:], ones[:], ba[:, 512 * j:512 * j + 512], start=False, stop=True).then_inc(f_filled, 1)
                bank = use(s, 9)
                for k in range(2):
                    mm = nc.tensor.matmul(bank[0:H, 0:P], wbeta[:, k, :], xnT[:, g, k, :], start=k == 0, stop=k == 1)
                mm.then_inc(f_filled, 1)

            def slot(s, n, g, lo, hi):
                if updates(lo - 1, hi - 1):
                    update(s - 1, n - 1 + g, 1 - g)
                if valid(lo + 1, hi + 1):
                    front2(s + 1, n + g, 1 - g)
                    products(s + 1, n + g, 1 - g)
                if valid(lo + 2, hi + 2):
                    front1(s + 2, n + 1, g)

            slot_loop(pe, slot, FIRST, LAST, LOOP)

        @block.scalar
        def _(act):
            act.wait_ge(init_done, 1)

            def filled(s, k):
                act.wait_ge(f_filled, F_USES * s + k + 1)
                return f_bank[k % F_BANKS]

            def sigmoids(s, n, g):
                if due(dma_of(v_wr, n, g, -1)[1]):
                    act.wait_ge(*dma_of(v_wr, n, g, -1))
                act.wait_ge(*dma_of(a_wr, n, g, 0))
                for j in range(3):
                    act.wait_ge(conv_chain, CONV_OPS * s + CONV_OPS // 3 * (j + 1))
                    if due(3 * s + j - 1):
                        act.wait_ge(silu_done, 3 * s + j - 1)
                    nc.scalar.activation(sg[:, j % 2], z[:, HP * j:HP * j + HP, :], ACT.Sigmoid,
                                         scale=float(DK) ** 0.5 if j == 1 else 1.0).then_inc(sg_ready, 1)

            def front2(s, n, g):
                act.wait_ge(silu_done, 3 * s + 2)
                if due(8 * (s - 1)):
                    act.wait_ge(p_filled, 8 * (s - 1))
                nc.scalar.activation(st[g][:, :, :, DV:DV + C], z[:, HP:2 * HP, :].rearrange("p h (b t) -> p b h t", b=GB),
                                     ACT.Copy).then_inc(keys_placed, 1)
                if due(8 * (s - 1)):
                    act.wait_ge(d_filled, 8 * (s - 1))
                for j in range(4):
                    bank = filled(s, F1_USES + j)
                    dst = kt[:, g] if j < 2 else vt
                    nc.scalar.activation(dst[:, 512 * (j % 2):512 * (j % 2) + 512], bank[:], ACT.Copy).then_inc(f_freed, 1)
                act.wait_ge(f_freed, F_USES * (s + 1))
                if due(dma_of(vb_in, n, g, -2)[1]):
                    act.wait_ge(*dma_of(vb_in, n, g, -2))
                act.dma_start(v_dram[g].rearrange("t b h i -> b t (h i)"), vt).then_inc(v_wr[g], 16)

            def products(s, n, g):
                if due(dma_of(p_wr, n, g, -1)[1]):
                    act.wait_ge(*dma_of(p_wr, n, g, -1))
                for b in range(GB):
                    act.wait_ge(p_filled, 8 * s + b + 1)
                    nc.scalar.activation(prod[:, b, :], p_bank[b % 2][:, 0:4 * ROW], ACT.Copy).then_inc(p_freed, 1)
                act.wait_ge(p_freed, 8 * s + 8)
                if due(dma_of(qp_in, n, g, -2)[1]):
                    act.wait_ge(*dma_of(qp_in, n, g, -2))
                if due(dma_of(kp_in, n, g, -2)[1]):
                    act.wait_ge(*dma_of(kp_in, n, g, -2))
                act.dma_start(prod_dram[g].rearrange("m p c -> p m c"), prod.rearrange("p b (q c) -> p (b q) c", c=ROW)).then_inc(p_wr[g], 16)

            def front1(s, n, g):
                if due(3 * s):
                    act.wait_ge(silu_done, 3 * s)
                if due(F_USES * s):
                    act.wait_ge(f_filled, F_USES * s)
                nc.scalar.activation(y[:, :, :, 0:TAPS - 1], halo[:, g], ACT.Copy).then_inc(halo_done, 1)
                act.wait_ge(halo_done, s + 1)
                bank = filled(s, 0)
                nc.scalar.activation(xnT[:, g].rearrange("p k t -> p (k t)"), bank[:, 0:2 * P], ACT.Copy).then_inc(f_freed, 1)
                for j in range(6):
                    bank = filled(s, 1 + j)
                    now = bank[:].rearrange("p (m b t) -> p m b t", m=4, b=GB)
                    for i in range(4):
                        m = 4 * j + i
                        nc.scalar.activation(z[:, m, :], bank[:, 128 * i:128 * i + 128], ACT.Identity,
                                             bias=conv_b[:, m:m + 1], scale=conv_w[:, m, TAPS - 1:TAPS])
                    nc.scalar.activation(halo[:, g, 4 * j:4 * j + 4], now[:, :, :, C - TAPS + 1:], ACT.Copy)
                    nc.scalar.activation(y[:, 4 * j:4 * j + 4, :, TAPS - 1:], now, ACT.Copy).then_inc(f_freed, 1)
                for j in range(2):
                    bank = filled(s, 7 + j)
                    nc.scalar.activation(at[:, 512 * j:512 * j + 512], bank[:], ACT.Sigmoid).then_inc(f_freed, 1)
                act.wait_ge(f_freed, F_USES * s + 9)
                if due(dma_of(ab_in, n, g, -2)[1]):
                    act.wait_ge(*dma_of(ab_in, n, g, -2))
                act.dma_start(a_dram[g].rearrange("t b h i -> b t (h i)"), at).then_inc(a_wr[g], 16)
                bank = filled(s, 9)
                if due(dma_of(beta_wr, n, g, -1)[1]):
                    act.wait_ge(*dma_of(beta_wr, n, g, -1))
                nc.scalar.activation(bt[:, 0], bank[0:H, 0:P], ACT.Sigmoid, bias=bb[:]).then_inc(f_freed, 1)
                act.wait_ge(f_freed, F_USES * s + 10)
                nc.scalar.activation(bt[:, 1], bt[:, 0], ACT.Copy, scale=-1.0).then_inc(bneg_done, 1)
                act.wait_ge(bneg_done, s + 1)
                if due(dma_of(nb_in, n, g, -2)[1]):
                    act.wait_ge(*dma_of(nb_in, n, g, -2))
                act.dma_start(beta_dram[g].rearrange("b h t -> h b t"), bt[:, 1].rearrange("h (b t) -> h b t", b=GB)).then_inc(beta_wr[g], 16)

            def slot(s, n, g, lo, hi):
                if valid(lo + 1, hi + 1):
                    sigmoids(s + 1, n + g, 1 - g)
                    front2(s + 1, n + g, 1 - g)
                    products(s + 1, n + g, 1 - g)
                if valid(lo + 2, hi + 2):
                    front1(s + 2, n + 1, g)

            slot_loop(act, slot, FIRST, LAST, LOOP)

        @block.vector
        def _(dve):
            for g in range(2):
                nc.vector.memset(st[g][:, :, :, 0:DV], 0.0)
            nc.vector.memset(xd[:], 0.0)
            nc.vector.memset(ones[:], 1.0)
            nc.vector.memset(halo[:], 0.0)
            dve.wait_ge(consts_in, 16 * 7)
            nc.vector.tensor_scalar(conv_w[:, HP:2 * HP, :], conv_w[:, HP:2 * HP, :], float(DK) ** -0.5, None, ALU.mult)
            nc.vector.tensor_scalar(conv_b[:, HP:2 * HP], conv_b[:, HP:2 * HP], float(DK) ** -0.5, None, ALU.mult).then_inc(init_done, 1)
            dve.wait_ge(init_done, 1)

            def conv(s, n, g):
                done = 0
                for j in range(6):
                    dve.wait_ge(f_freed, F_USES * s + j + 2)
                    for tap in range(TAPS - 1):
                        for i in range(4):
                            m = 4 * j + i
                            if tap:
                                dve.wait_ge(conv_chain, CONV_OPS * s + done - 3)
                            zz = z[:, m, :].rearrange("p (b t) -> p b t", b=GB)
                            nc.vector.scalar_tensor_tensor(
                                out=zz, in0=y[:, m, :, tap:tap + C], scalar=conv_w[:, m, tap:tap + 1], in1=zz,
                                op0=ALU.mult, op1=ALU.add).then_inc(conv_chain, 1)
                            done += 1
                assert done == CONV_OPS

            def silu(s, n, g):
                if due(8 * (s - 1)):
                    dve.wait_ge(p_filled, 8 * (s - 1))
                for j in range(3):
                    dve.wait_ge(sg_ready, 3 * s + j + 1)
                    v = z[:, HP * j:HP * j + HP, :]
                    if j == 0:
                        nc.vector.tensor_tensor(st[g][:, :, :, DV + C:DV + 2 * C], v.rearrange("p h (b t) -> p b h t", b=GB),
                                                sg[:, 0].rearrange("p h (b t) -> p b h t", b=GB),
                                                ALU.mult).then_inc(silu_done, 1)
                    else:
                        nc.vector.tensor_tensor(v, v, sg[:, j % 2], ALU.mult).then_inc(silu_done, 1)

            def state(s, n, g):
                dve.wait_ge(*dma_of(db_in, n, g, 0, 32))
                dve.wait_ge(p_filled, 8 * (s + 1))
                sv = st[g][:, :, :, 0:DV]
                nc.vector.tensor_tensor(sv.rearrange("p b h i -> p (b h) i"), sv.rearrange("p b h i -> p (b h) i"), db[:],
                                        ALU.mult).then_inc(decayed, 1)
                dve.wait_ge(decayed, s + 1)
                for u in range(8):
                    q, hh = u // 2, u % 2
                    dve.wait_ge(d_filled, 8 * s + u + 1)
                    part = st[g][:, 2 * q:2 * q + 2, 4 * hh:4 * hh + 4, 0:DV]
                    nc.vector.tensor_tensor(part, d_bank[u % 2][:].rearrange("p (h b i) -> p b h i", h=4, b=2), part,
                                            ALU.add).then_inc(d_freed, 1)

            def norm(s, n, g):
                base, made = (3 + RSQRT_OPS) * s, [0]

                def link(ins):
                    made[0] += 1
                    ins.then_inc(norm_chain, 1)
                    dve.wait_ge(norm_chain, base + made[0])

                dve.wait_ge(x_in[g], 16 * (n + 1))
                link(nc.vector.bn_stats(bst[:], xt[:, g, :]))
                held(dve, dve_passed)
                link(nc.vector.bn_aggr(mv[:], bst[:]))
                link(nc.vector.tensor_scalar(var[:], mv[:, 1:2], EPS, None, ALU.add))
                rsqrt_ops(nc, rs[:], var[:], rstmp[:], link)
                if due(F_USES * (s - 1) + 1):
                    dve.wait_ge(f_filled, F_USES * (s - 1) + 1)
                nc.vector.tensor_scalar(xn[:], xt[:, g, :], mv[:, 0:1], rs[:], ALU.subtract, ALU.mult).then_inc(xn_ready, 1)

            def solve(s, n, g):
                base, made = SOLVE_OPS * s, [0]

                def link(ins):
                    made[0] += 1
                    ins.then_inc(solve_chain, 1)
                    dve.wait_ge(solve_chain, base + made[0])

                dve.wait_ge(*dma_of(qp_in, n, g, 0))
                dve.wait_ge(*dma_of(kp_in, n, g, 0))
                dve.wait_ge(*dma_of(vb_in, n, g, 0))
                dve.wait_ge(*dma_of(ab_in, n, g, 0))
                dve.wait_ge(*dma_of(nb_in, n, g, 0))
                for dots in (qp[:, g, :, DV:ROW], kp[:, :, DV:ROW]):
                    link(nc.vector.tensor_tensor(dots, dots, nb[:, g:g + 1, :].to_broadcast([128, C, C]), ALU.mult))
                for r in range(C):
                    w = C - 1 - r
                    rows = kp[:, r + 1:C, 0:DV]
                    link(nc.vector.tensor_tensor(vb[:, g, r, :], kp[:, r, 0:DV], vb[:, g, r, :], ALU.subtract))
                    if w:
                        link(nc.vector.tensor_tensor(rows, rows, ab[:, g, r:r + 1, :].to_broadcast([128, w, DV]), ALU.mult))
                        link(nc.vector.tensor_tensor(
                            t2[:, 0:w], kp[:, r + 1:C, DV + r:DV + r + 1].to_broadcast([128, w, DV]),
                            vb[:, g, r:r + 1, :].to_broadcast([128, w, DV]), ALU.mult))
                        link(nc.vector.tensor_tensor(rows, rows, t2[:, 0:w], ALU.add))
                dve.wait_ge(pool_chain, POOL_OPS * s + DECAY_OPS + 2)
                link(nc.vector.tensor_tensor(eb[:], vb[:, g], eb[:], ALU.mult))
                assert made[0] == SOLVE_OPS

            def slot(s, n, g, lo, hi):
                if valid(lo + 1, hi + 1):
                    conv(s + 1, n + g, 1 - g)
                    silu(s + 1, n + g, 1 - g)
                if updates(lo - 1, hi - 1):
                    state(s - 1, n - 1 + g, 1 - g)
                if valid(lo + 2, hi + 2):
                    norm(s + 2, n + 1, g)
                if valid(lo, hi):
                    solve(s, n, g)

            slot_loop(dve, slot, FIRST, LAST, LOOP)


WORK_BANKS = 3


def turn_uses(attention, tiles):
    uses = []
    for j in range(NT):
        if attention:
            uses += [("score", j, t, i) for t in range(NT) for i in range(4)] + [("max", j)]
        if tiles:
            uses += [("xn", j), ("gate", j, 0), ("gate", j, 1), ("small", j), ("lora", j), ("og", j, 0), ("og", j, 1),
                     ("x1", j)]
        if attention:
            uses += [("heads", j)]
    if attention:
        uses += [("joined", t) for t in range(NT // 2)] + [("out", t) for t in range(NT)]
    if tiles:
        uses += [("xn2", k) for k in range(2)] + [("qk", m) for m in range(2 * HG)] + [("v", t) for t in range(NT // 2)]
        uses += [("rest", t) for t in range(NT // 2)]
    return uses


class Turn:

    def __init__(self, b, attention, tiles):
        names = turn_uses(attention, tiles)
        self.place, count = {}, [0] * WORK_BANKS
        for n, name in enumerate(names):
            bank = n % WORK_BANKS
            self.place[name] = bank, count[bank]
            count[bank] += 1
        first, full = ([len(turn_uses(*w)[k::WORK_BANKS]) for k in range(WORK_BANKS)] for w in ((False, True), (True, True)))
        self.before = [0] * WORK_BANKS if not attention else [first[k] + full[k] * b for k in range(WORK_BANKS)]

    def count(self, name):
        bank, n = self.place[name]
        return bank, self.before[bank] + n


def turns(engine, body):
    body(-1, Turn(-1, False, True), False, True)
    body(0, Turn(0, True, True), True, True)
    with engine.Fori(1, B - 1) as b:
        body(b, Turn(b, True, True), True, True)
    body(B - 1, Turn(B - 1, True, False), True, False)


def layer0_end_and_layer1(nc, ins, o_dram, out):
    x = ins["L0_attn_x"]
    with ExitStack() as ctx:
        def sb(name, shape, dt=f32):
            return ctx.enter_context(nc.sbuf_tensor(name, shape, dt))

        def ps(name, shape):
            return ctx.enter_context(nc.psum_tensor(name, shape, f32))

        def sem(name):
            return ctx.enter_context(nc.semaphore(name))

        ident = sb("ident2", [128, 128])
        ones = sb("ones2", [1, 128])
        iota = sb("iota", [128, E])
        wg = sb("wg", [128, 2, HD])
        wsm = sb("wsm", [128, 2, E + ER])
        wbase = sb("wbase", [128, 2, HID])
        wo = sb("wo", [128, HP, HID])
        lup = sb("lup", [ER, HID])
        gate_b = sb("gate_b", [1, E + ER])
        b_base = sb("b_base", [1, HID])
        ln_w = sb("ln_w", [128, DV])
        ln_b = sb("ln_b", [128, DV])
        wqk = sb("wqk", [128, 2, 2 * HG, 128])
        bqk = sb("bqk", [128, 2 * HG])
        wv = sb("wv", [128, 2, HID])
        bv = sb("bv", [128, HID])
        w_out = sb("w_out", [128, 2, HID])
        b_out = sb("b_out", [1, HID])
        bias = sb("bias", [1, HID])
        kern = sb("kern", [128, 2, HID])
        aT = sb("aT", [16, HID])
        bmat = sb("bmat", [16, HID])
        wffn = sb("wffn", [128, 2, HID])
        pmax = sb("pmax", [128, 1])
        pmaxT = sb("pmaxT", [1, 128])
        gmax = sb("gmax", [1, 1])
        scale = sb("scale", [128, 2])

        px = sb("px", [128, 2, HID])
        ot = sb("ot", [128, 2, H, DV])
        xn = sb("xn_b", [128, HID])
        xnT = sb("xnT_b", [128, 2, 128])
        gl = sb("gl", [128, H, DV])
        lh = sb("lh", [128, E + ER])
        hw = sb("hw", [128, ER])
        hwT = sb("hwT", [ER, 128])
        top = sb("top", [128, 8])
        topi = sb("topi", [128, 8], u32)
        topf = sb("topf", [128, 2])
        dtop = sb("dtop", [128, 1])
        topt = sb("topt", [128, 2])
        topw = sb("topw", [128, 2])
        wexp = sb("wexp", [128, 2, E])
        ogT = sb("ogT", [128, HP, 128])
        bst = sb("bst_b", [128, H + 1, 6])
        mv = sb("mv_b", [128, 2])
        m2 = sb("m2", [128, H])
        dm = sb("dm", [128, H])
        vs = sb("vs", [128, H])
        var = sb("var_b", [128, H + 1])
        rs = sb("rs_b", [128, H + 1])
        rstmp = sb("rstmp_b", [128, H + 1])
        nmr = sb("nmr", [128, H])
        x1 = sb("x1", [128, NT, HID])

        bst2 = sb("bst2", [128, NT, 6])
        mv2 = sb("mv2", [128, NT, 2])
        var2 = sb("var2", [128, NT])
        rs2 = sb("rs2", [128, NT])
        rstmp2 = sb("rstmp2", [128, NT])
        xn2 = sb("xn2", [128, NT, HID])
        xn2T = sb("xn2T", [128, 2, T])
        qk = sb("qk", [128, 2 * HG, T])
        v = sb("v", [128, NT, H1, 32])
        rest = sb("rest", [128, NT, HID])
        nmax = sb("nmax", [128, NT, 128])
        qa = sb("qa", [128, T])
        pt = sb("pt", [128, 2, 2, T])
        oa = sb("oa", [128, T])
        rden = sb("rden", [128, NT * 4])
        mark = sb("mark", [128, 8])
        ao = sb("ao", [128, NT, H1, D1])
        aoT = sb("aoT", [128, 2, T])
        ob = sb("ob", [128, 2, HID])

        w_bank = [ps(f"w_bank{i}", [128, 512]) for i in range(WORK_BANKS)]
        e_bank = [ps(f"e_bank{i}", [128, 2, 512]) for i in range(2)]
        o_bank = ps("o_bank", [128, 512])

        consts_in, ident_done, init_done, init_chain, init_pe, init_act = map(
            sem, ("consts_in2", "ident_done2", "init_done2", "init_chain", "init_pe", "init_act"))
        w_filled = [sem(f"w_filled{i}") for i in range(WORK_BANKS)]
        w_freed = [sem(f"w_freed{i}") for i in range(WORK_BANKS)]
        px_in, ot_in = [sem(f"px_in{i}") for i in range(2)], [sem(f"ot_in{i}") for i in range(2)]
        stat_chain, tile_ready, gate_chain, gates_tanh, normed, affine = map(
            sem, ("stat_chain", "tile_ready", "gate_chain", "gates_tanh", "normed", "affine"))
        affine_chain, og_done, x1_done, lh_done = map(sem, ("affine_chain", "og_done", "x1_done", "lh_done"))
        hw_ready, xn2_chain, xn2_ready, qa_ready, nmax_ready = map(
            sem, ("hw_ready", "xn2_chain", "xn2_ready", "qa_ready", "nmax_ready"))
        e_filled, e_freed, o_filled, o_freed, pv_done = map(sem, ("e_filled", "e_freed", "o_filled", "o_freed", "pv_done"))
        oa_done, heads_done, rden_done = map(sem, ("oa_done", "heads_done", "rden_done"))
        out_wr = [sem(f"out_wr{i}") for i in range(2)]
        sp_passed, pe_passed, dve_passed = map(sem, ("sp_passed2", "pe_passed2", "dve_passed2"))
        CONSTS = 20
        STAT_OPS = 3 + 7 + 14
        GATE_OPS = 8
        XN2_OPS = 2 * NT + 1 + 14

        block = ctx.enter_context(nc.Block())

        @block.sync
        def _(sp):
            def row(a):
                return a.rearrange("(a n) -> a n", a=1)

            def tiles(a):
                return a.rearrange("(k p) n -> p k n", p=128)

            loads = (
                (wg[:], tiles(ins["wg"])), (wsm[:], tiles(ins["wsm"])), (wbase[:], tiles(ins["wbase"])),
                (wo[:], tiles(ins["wo"])), (lup[:], ins["lup"]), (gate_b[:, 0:E], row(ins["L0_ffn_gate_b"])),
                (b_base[:], row(ins["L0_ffn_b_base"])),
                (ln_w[:], row(ins["L0_attn_ln_w"]).to_broadcast([128, DV])),
                (ln_b[:], row(ins["L0_attn_ln_b"]).to_broadcast([128, DV])),
                (wqk[:], ins["wqk"].rearrange("(k p) m n -> p k m n", p=128)), (bqk[:], ins["bqk"]),
                (wv[:], tiles(ins["wv"])), (bv[:], row(ins["bv"]).to_broadcast([128, HID])),
                (w_out[:], tiles(ins["L1_attn_w_out"])), (b_out[:], row(ins["L1_attn_b_out"])),
                (bias[:], row(ins["L1_ffn_bias"])), (kern[:], tiles(ins["L1_ffn_kernel"])),
                (aT[:], ins["aT"]), (bmat[:], ins["L1_ffn_b"]),
            )
            for tile, src in loads:
                sp.dma_start(tile, src).then_inc(consts_in, 16)
            assert len(loads) == CONSTS - 1

            def body(b, turn, attention, tiles_):
                for j in range(NT):
                    if tiles_:
                        bt = b + 1
                        if due(NT * bt + j - 1):
                            sp.wait_ge(x1_done, NT * bt + j - 1)
                        held(sp, sp_passed)
                        sp.dma_start(px[:, j % 2], x[bass.ds(bt, 1), 128 * j:128 * j + 128]).then_inc(px_in[j % 2], 16)
                        sp.dma_start(ot[:, j % 2], o_dram[128 * j:128 * j + 128, bass.ds(bt, 1)]).then_inc(ot_in[j % 2], 16)
            turns(sp, body)

        @block.gpsimd
        def _(pool):
            nc.gpsimd.memset(ident[:], 0.0).then_inc(ident_done, 1)
            pool.wait_ge(ident_done, 1)
            nc.gpsimd.affine_select(out=ident[:], in_=ident[:], compare_op=ALU.not_equal, fill=1.0, base=0,
                                    pattern=[[-1, 128]], channel_multiplier=1).then_inc(ident_done, 1)
            pool.wait_ge(init_done, 1)

            def body(b, turn, attention, tiles_):
                for j in range(NT):
                    if tiles_:
                        t = NT * (b + 1) + j
                        o = ot[:, j % 2]
                        pool.wait_ge(normed, t + 1)
                        nc.gpsimd.tensor_tensor(o, o, ln_w[:].unsqueeze(1).to_broadcast([128, H, DV]), ALU.mult).then_inc(affine_chain, 1)
                        pool.wait_ge(affine_chain, t + 1)
                        nc.gpsimd.tensor_tensor(o, o, ln_b[:].unsqueeze(1).to_broadcast([128, H, DV]), ALU.add).then_inc(affine, 1)
            turns(pool, body)

        @block.tensor
        def _(pe):
            pe.wait_ge(consts_in, 16 * (CONSTS - 1))
            pe.wait_ge(ident_done, 2)
            pe.wait_ge(init_chain, 1)
            nc.tensor.transpose(w_bank[0][0:1, 0:128], pmax[:], ident[:]).then_inc(init_pe, 1)
            pe.wait_ge(init_chain, 3)
            nc.tensor.matmul(w_bank[1][:, 0:1], ones[:], gmax[:], start=True, stop=True).then_inc(init_pe, 1)
            for k in range(2):
                mm = nc.tensor.matmul(w_bank[2][:, HID * k:HID * k + HID], aT[:, 128 * k:128 * k + 128], bmat[:], start=True, stop=True)
            mm.then_inc(init_pe, 1)
            pe.wait_ge(init_done, 1)

            def body(b, turn, attention, tiles_):
                def use(*name):
                    bank, n = turn.count(name)
                    if due(n):
                        pe.wait_ge(w_freed[bank], n)
                    return w_bank[bank], w_filled[bank]

                def attend(j):
                    for t in range(NT):
                        for i in range(4):
                            bank, filled = use("score", j, t, i)
                            nc.tensor.matmul(bank[:], qk[32 * i:32 * i + 32, j, 128 * t:128 * t + 128],
                                             qk[32 * i:32 * i + 32, HG + j, :], start=True, stop=True,
                                             tile_position=(32 * i, 0)).then_inc(filled, 1)
                    bank, filled = use("max", j)
                    pe.wait_ge(nmax_ready, 16 * (NT * b + j + 1))
                    for t in range(NT):
                        mm = nc.tensor.transpose(bank[:, 128 * t:128 * t + 128], nmax[:, t, :], ident[:])
                    mm.then_inc(filled, 1)
                    pe.wait_ge(qa_ready, NT * b + j + 1)

                    def context(half):
                        c = 2 * NT * (NT * b + j)
                        kt, pr = half // 2, half % 2
                        pe.wait_ge(e_freed, c + half + 1)
                        for i in (2 * pr, 2 * pr + 1):
                            mm = nc.tensor.matmul(o_bank[32 * i:32 * i + 32, :], v[:, kt, 4 * j + i, :], pt[:, pr, i % 2, :],
                                                  start=kt == 0, stop=kt == NT - 1, tile_position=(0, 32 * i))
                        mm.then_inc(pv_done, 1)

                    for half in range(2 * NT):
                        kt, pr = half // 2, half % 2
                        if half >= 2:
                            pe.wait_ge(e_freed, 2 * NT * (NT * b + j) + half - 1)
                        for i in (2 * pr, 2 * pr + 1):
                            mm = nc.tensor.matmul(e_bank[pr][:, i % 2, :], qk[32 * i:32 * i + 32, HG + j, 128 * kt:128 * kt + 128],
                                                  qa[32 * i:32 * i + 32, :], start=True, stop=True, tile_position=(32 * i, 0))
                        mm.then_inc(e_filled, 1)
                        if half == 0:
                            if due(NT * b + j):
                                pe.wait_ge(o_freed, NT * b + j)
                        else:
                            context(half - 1)
                    context(2 * NT - 1)

                def heads(j):
                    bank, filled = use("heads", j)
                    pe.wait_ge(oa_done, NT * b + j + 1)
                    for t in range(NT):
                        mm = nc.tensor.transpose(bank[:, 128 * t:128 * t + 128], oa[:, 128 * t:128 * t + 128], ident[:])
                    mm.then_inc(filled, 1)

                def tile(j):
                    t = NT * (b + 1) + j
                    bank, filled = use("xn", j)
                    pe.wait_ge(tile_ready, t + 1)
                    for k in range(2):
                        mm = nc.tensor.transpose(bank[:, 128 * k:128 * k + 128], xn[:, 128 * k:128 * k + 128], ident[:])
                    mm.then_inc(filled, 1)
                    bk, n = turn.count(("xn", j))
                    pe.wait_ge(w_freed[bk], n + 1)
                    for h in range(2):
                        bank, filled = use("gate", j, h)
                        for k in range(2):
                            mm = nc.tensor.matmul(bank[:], xnT[:, k, :], wg[:, k, 512 * h:512 * h + 512], start=k == 0, stop=k == 1)
                        mm.then_inc(filled, 1)
                    bank, filled = use("small", j)
                    for k in range(2):
                        nc.tensor.matmul(bank[:, 0:E + ER], xnT[:, k, :], wsm[:, k, :], start=k == 0, stop=False)
                    nc.tensor.matmul(bank[:, 0:E + ER], ones[:], gate_b[:], start=False, stop=True).then_inc(filled, 1)
                    bank, filled = use("lora", j)
                    pe.wait_ge(hw_ready, t + 1)
                    held(pe, pe_passed)
                    nc.tensor.transpose(bank[0:ER, 0:128], hw[:], ident[:]).then_inc(filled, 1)
                    for h in range(2):
                        bank, filled = use("og", j, h)
                        pe.wait_ge(og_done, t + 1)
                        for i in range(4):
                            m = 4 * h + i
                            mm = nc.tensor.transpose(bank[:, 128 * i:128 * i + 128], ot[:, j % 2, 2 * m:2 * m + 2, :].rearrange("p h i -> p (h i)"), ident[:])
                        mm.then_inc(filled, 1)
                    bank, filled = use("x1", j)
                    for last in (("lora", j), ("og", j, 0), ("og", j, 1)):
                        bk, n = turn.count(last)
                        pe.wait_ge(w_freed[bk], n + 1)
                    for k in range(2):
                        nc.tensor.matmul(bank[:, 0:HID], xnT[:, k, :], wbase[:, k, :], start=k == 0, stop=False)
                    nc.tensor.matmul(bank[:, 0:HID], ones[:], b_base[:], start=False, stop=False)
                    nc.tensor.matmul(bank[:, 0:HID], hwT[:], lup[:], start=False, stop=False)
                    for m in range(HP):
                        nc.tensor.matmul(bank[:, 0:HID], ogT[:, m, :], wo[:, m, :], start=False, stop=False)
                    nc.tensor.matmul(bank[:, 0:HID], ident[:], px[:, j % 2], start=False, stop=True).then_inc(filled, 1)

                for j in range(NT):
                    if attention:
                        attend(j)
                    if tiles_:
                        tile(j)
                    if attention:
                        heads(j)
                if attention:
                    pe.wait_ge(heads_done, NT * (b + 1))
                    for t in range(NT // 2):
                        bank, filled = use("joined", t)
                        for i in range(2):
                            for k in range(2):
                                mm = nc.tensor.transpose(bank[:, 256 * i + 128 * k:256 * i + 128 * k + 128],
                                                         ao[:, 2 * t + i].rearrange("p h d -> p (h d)")[:, 128 * k:128 * k + 128], ident[:])
                        mm.then_inc(filled, 1)
                    for t in range(NT):
                        bank, filled = use("out", t)
                        bk, n = turn.count(("joined", t // 2))
                        pe.wait_ge(w_freed[bk], n + 1)
                        for k in range(2):
                            nc.tensor.matmul(bank[:, 0:HID], aoT[:, k, 128 * t:128 * t + 128], w_out[:, k, :], start=k == 0, stop=False)
                        nc.tensor.matmul(bank[:, 0:HID], ident[:], rest[:, t, :], start=False, stop=True).then_inc(filled, 1)
                if tiles_:
                    pe.wait_ge(xn2_ready, NT * (b + 2))
                    for k in range(2):
                        bank, filled = use("xn2", k)
                        for t in range(NT):
                            mm = nc.tensor.transpose(bank[:, 128 * t:128 * t + 128], xn2[:, t, 128 * k:128 * k + 128], ident[:])
                        mm.then_inc(filled, 1)
                    for k in range(2):
                        bk, n = turn.count(("xn2", k))
                        pe.wait_ge(w_freed[bk], n + 1)
                    for m in range(2 * HG):
                        bank, filled = use("qk", m)
                        for k in range(2):
                            mm = nc.tensor.matmul(bank[:], wqk[:, k, m, :], xn2T[:, k, :], start=k == 0, stop=k == 1)
                        mm.then_inc(filled, 1)
                    for t in range(NT // 2):
                        bank, filled = use("v", t)
                        for i in range(2):
                            for k in range(2):
                                mm = nc.tensor.matmul(bank[:, HID * i:HID * i + HID], xn2T[:, k, 128 * (2 * t + i):128 * (2 * t + i) + 128],
                                                      wv[:, k, :], start=k == 0, stop=k == 1)
                        mm.then_inc(filled, 1)
                    for t in range(NT // 2):
                        bank, filled = use("rest", t)
                        for i in range(2):
                            part = bank[:, HID * i:HID * i + HID]
                            for k in range(2):
                                nc.tensor.matmul(part, xn2T[:, k, 128 * (2 * t + i):128 * (2 * t + i) + 128], wffn[:, k, :], start=k == 0, stop=False)
                            nc.tensor.matmul(part, ones[:], b_out[:], start=False, stop=False)
                            mm = nc.tensor.matmul(part, ones[:], bias[:], start=False, stop=True)
                        mm.then_inc(filled, 1)
            turns(pe, body)

        @block.scalar
        def _(act):
            act.wait_ge(init_done, 1)

            def body(b, turn, attention, tiles_):
                def filled(*name):
                    bank, n = turn.count(name)
                    act.wait_ge(w_filled[bank], n + 1)
                    return w_bank[bank], w_freed[bank]

                def attend(j):
                    for half in range(2 * NT):
                        c = 2 * NT * (NT * b + j) + half
                        act.wait_ge(e_filled, c + 1)
                        if half >= 2:
                            act.wait_ge(pv_done, c - 1)
                        nc.scalar.activation(pt[:, half % 2], e_bank[half % 2][:], ACT.Exp, scale=float(D1) ** -0.5).then_inc(e_freed, 1)
                    act.wait_ge(pv_done, 2 * NT * (NT * b + j + 1))
                    bank, n = turn.count(("heads", j))
                    nc.scalar.activation(oa[:], o_bank[:], ACT.Copy).then_inc(oa_done, 1)
                    act.wait_ge(oa_done, NT * b + j + 1)
                    nc.scalar.activation(mark[:, 0:1], mark[:, 1:2], ACT.Copy).then_inc(o_freed, 1)

                def tile(j):
                    t = NT * (b + 1) + j
                    bank, freed = filled("xn", j)
                    nc.scalar.activation(xnT[:].rearrange("p k t -> p (k t)"), bank[:, 0:256], ACT.Copy).then_inc(freed, 1)
                    if due(t):
                        act.wait_ge(og_done, t)
                    for h in range(2):
                        bank, freed = filled("gate", j, h)
                        nc.scalar.activation(gl[:, 8 * h:8 * h + 8].rearrange("p h i -> p (h i)"), bank[:], ACT.Tanh, scale=0.5).then_inc(freed, 1)
                    bank, freed = filled("small", j)
                    if due(t):
                        act.wait_ge(hw_ready, t)
                    nc.scalar.activation(lh[:], bank[:, 0:E + ER], ACT.Copy).then_inc(freed, 1)
                    o = ot[:, j % 2]
                    for h in range(H):
                        norm_ = nc.scalar.activation(o[:, h, :], o[:, h, :], ACT.Identity, bias=nmr[:, h:h + 1], scale=rs[:, h + 1:h + 2])
                    norm_.then_inc(normed, 1)
                    act.wait_ge(gate_chain, GATE_OPS * t + 4)
                    nc.scalar.activation(topt[:, 0:1], dtop[:], ACT.Tanh, scale=-0.5)
                    nc.scalar.activation(topt[:, 1:2], dtop[:], ACT.Tanh, scale=0.5).then_inc(gates_tanh, 1)
                    bank, freed = filled("lora", j)
                    nc.scalar.activation(hwT[:], bank[0:ER, 0:128], ACT.Copy).then_inc(freed, 1)
                    for h in range(2):
                        bank, freed = filled("og", j, h)
                        nc.scalar.activation(ogT[:, 4 * h:4 * h + 4].rearrange("p m t -> p (m t)"), bank[:], ACT.Copy).then_inc(freed, 1)
                    bank, freed = filled("x1", j)
                    if due(NT * (b + 1)):
                        act.wait_ge(xn2_ready, NT * (b + 1))
                    bk, n = turn.count(("x1", j))
                    nc.scalar.activation(x1[:, j, :], bank[:, 0:HID], ACT.Copy).then_inc(freed, 1)
                    act.wait_ge(freed, n + 1)
                    nc.scalar.activation(mark[:, 2:3], mark[:, 1:2], ACT.Copy).then_inc(x1_done, 1)

                for j in range(NT):
                    if attention:
                        attend(j)
                    if tiles_:
                        tile(j)
                if attention:
                    for t in range(NT // 2):
                        bank, freed = filled("joined", t)
                        nc.scalar.activation(aoT[:, :, 256 * t:256 * t + 256].rearrange("p k (i q) -> p i k q", i=2),
                                             bank[:].rearrange("p (i k q) -> p i k q", i=2, k=2), ACT.Copy).then_inc(freed, 1)
                    for t in range(NT):
                        bank, freed = filled("out", t)
                        if due(16 * (2 * b + t // 2)):
                            act.wait_ge(out_wr[t % 2], 16 * (2 * b + t // 2))
                        nc.scalar.activation(ob[:, t % 2], bank[:, 0:HID], ACT.Copy).then_inc(freed, 1)
                        bk, n = turn.count(("out", t))
                        act.wait_ge(freed, n + 1)
                        act.dma_start(out[bass.ds(b, 1), 128 * t:128 * t + 128], ob[:, t % 2]).then_inc(out_wr[t % 2], 16)
                if tiles_:
                    for k in range(2):
                        bank, freed = filled("xn2", k)
                        nc.scalar.activation(xn2T[:, k, :], bank[:], ACT.Copy).then_inc(freed, 1)
                    for m in range(2 * HG):
                        bank, freed = filled("qk", m)
                        nc.scalar.activation(qk[:, m, :], bank[:], ACT.Identity, bias=bqk[:, m:m + 1]).then_inc(freed, 1)
            turns(act, body)
            for i in range(2):
                act.wait_ge(out_wr[i], 16 * 2 * B)

        @block.vector
        def _(dve):
            chain = [0]

            def start(ins_):
                chain[0] += 1
                ins_.then_inc(init_chain, 1)
                dve.wait_ge(init_chain, chain[0])

            dve.wait_ge(consts_in, 16 * (CONSTS - 1))
            start(nc.vector.tensor_reduce(pmax[:], kern[:], AX.XY, ALU.max, apply_absolute_value=True))
            dve.wait_ge(init_pe, 1)
            start(nc.vector.memset(ones[:], 1.0))
            start(nc.vector.reduce_max(gmax[:], w_bank[0][0:1, 0:128], AX.X))
            dve.wait_ge(init_pe, 2)
            start(nc.vector.tensor_scalar(scale[:, 0:1], w_bank[1][:, 0:1], 1.0 / 7.0, None, ALU.mult))
            start(nc.vector.reciprocal(scale[:, 1:2], scale[:, 0:1]))
            start(nc.vector.tensor_scalar(wffn[:], kern[:], scale[:, 1:2], None, ALU.mult))
            start(nc.vector.tensor_scalar(wffn[:], wffn[:], ROUND, None, ALU.add))
            start(nc.vector.tensor_scalar(wffn[:], wffn[:], ROUND, -8.0, ALU.subtract, ALU.max))
            start(nc.vector.tensor_scalar(wffn[:], wffn[:], 7.0, scale[:, 0:1], ALU.min, ALU.mult))
            dve.wait_ge(init_pe, 3)
            start(nc.vector.tensor_tensor(wffn[:].rearrange("p k n -> p (k n)"), wffn[:].rearrange("p k n -> p (k n)"), w_bank[2][:], ALU.add))
            start(nc.vector.tensor_scalar(ln_w[:], ln_w[:], 0.5, None, ALU.mult))
            start(nc.vector.tensor_scalar(ln_b[:], ln_b[:], 0.5, None, ALU.mult))
            start(nc.vector.tensor_scalar(lup[:], lup[:], 1.0 / R, None, ALU.mult))
            start(nc.vector.memset(gate_b[:, E:], 0.0))
            start(nc.vector.memset(nmax[:], 0.0))
            start(nc.vector.memset(mark[:], 0.0))
            start(nc.vector.memset(v[:, :, :, D1:], 0.0))
            start(nc.vector.memset(v[:, :, :, D1:D1 + 1], 1.0))
            for e in range(E):
                nc.vector.memset(iota[:, e:e + 1], float(e))
            nc.vector.memset(rstmp[:], 0.0).then_inc(init_done, 1)
            dve.wait_ge(init_done, 1)

            def linker(sem_, base):
                made = [0]

                def link(ins_):
                    made[0] += 1
                    ins_.then_inc(sem_, 1)
                    dve.wait_ge(sem_, base + made[0])
                return link

            def body(b, turn, attention, tiles_):
                def filled(*name):
                    bank, n = turn.count(name)
                    dve.wait_ge(w_filled[bank], n + 1)
                    return w_bank[bank], w_freed[bank]

                def attend(j):
                    for t in range(NT):
                        for i in range(4):
                            bank, freed = filled("score", j, t, i)
                            if t == 0 and i == 0:
                                if due(NT * b + j):
                                    dve.wait_ge(qa_ready, NT * b + j)
                            nc.vector.tensor_reduce(nmax[:, t, 32 * i + D1:32 * i + D1 + 1], bank[:], AX.X, ALU.max, negate=True).then_inc(freed, 1)
                    nc.vector.memset(mark[:, 4:5], 0.0).then_inc(nmax_ready, 16)
                    bank, freed = filled("max", j)
                    if due(2 * NT * (NT * b + j)):
                        dve.wait_ge(e_filled, 2 * NT * (NT * b + j))
                    nc.vector.tensor_tensor(qa[:], bank[:], qk[:, j, :], ALU.add).then_inc(freed, 1)
                    bk, n = turn.count(("max", j))
                    dve.wait_ge(freed, n + 1)
                    nc.vector.memset(mark[:, 5:6], 0.0).then_inc(qa_ready, 1)

                def join(j):
                    bank, freed = filled("heads", j)
                    o = bank[:].rearrange("p (m c) -> p m c", c=32)
                    nc.vector.reciprocal(rden[:], o[:, :, D1]).then_inc(rden_done, 1)
                    dve.wait_ge(rden_done, NT * b + j + 1)
                    nc.vector.tensor_tensor(ao[:, :, 4 * j:4 * j + 4, :], o[:, :, 0:D1].rearrange("p (t i) d -> p t i d", t=NT),
                                            rden[:].rearrange("p (t i) -> p t i", t=NT).unsqueeze(3).to_broadcast([128, NT, 4, D1]),
                                            ALU.mult).then_inc(freed, 1)
                    bk, n = turn.count(("heads", j))
                    dve.wait_ge(freed, n + 1)
                    nc.vector.memset(mark[:, 6:7], 0.0).then_inc(heads_done, 1)

                def tile(j):
                    t = NT * (b + 1) + j
                    link = linker(stat_chain, STAT_OPS * t)
                    need_tile = 16 * (2 * (b + 1) + j // 2 + 1)
                    dve.wait_ge(px_in[j % 2], need_tile)
                    if due(t):
                        dve.wait_ge(normed, t)
                    link(nc.vector.bn_stats(bst[:, H, :], px[:, j % 2]))
                    held(dve, dve_passed)
                    link(nc.vector.bn_aggr(mv[:], bst[:, H, :]))
                    link(nc.vector.tensor_scalar(var[:, 0:1], mv[:, 1:2], EPS, None, ALU.add))
                    dve.wait_ge(ot_in[j % 2], need_tile)
                    for h in range(H):
                        last = nc.vector.bn_stats(bst[:, h, :], ot[:, j % 2, h, :])
                    link(last)
                    link(nc.vector.tensor_tensor(m2[:], bst[:, 0:H, 1], bst[:, 0:H, 4], ALU.add))
                    link(nc.vector.tensor_tensor(dm[:], bst[:, 0:H, 1], bst[:, 0:H, 4], ALU.subtract))
                    link(nc.vector.tensor_tensor(dm[:], dm[:], dm[:], ALU.mult))
                    link(nc.vector.tensor_tensor(vs[:], bst[:, 0:H, 2], bst[:, 0:H, 5], ALU.add))
                    link(nc.vector.scalar_tensor_tensor(out=vs[:], in0=dm[:], scalar=DV / 4.0, in1=vs[:], op0=ALU.mult, op1=ALU.add))
                    link(nc.vector.tensor_scalar(var[:, 1:], vs[:], 1.0 / DV, EPS, ALU.mult, ALU.add))
                    rsqrt_ops(nc, rs[:], var[:], rstmp[:], link)
                    bank, n = turn.count(("xn", j))
                    nc.vector.scalar_tensor_tensor(out=nmr[:], in0=m2[:], scalar=-0.5, in1=rs[:, 1:], op0=ALU.mult, op1=ALU.mult)
                    nc.vector.tensor_scalar(xn[:], px[:, j % 2], mv[:, 0:1], rs[:, 0:1], ALU.subtract, ALU.mult).then_inc(tile_ready, 1)
                    link = linker(gate_chain, GATE_OPS * t)
                    bk, n = turn.count(("small", j))
                    dve.wait_ge(w_freed[bk], n + 1)
                    held(dve, dve_passed)
                    link(nc.vector.max(top[:], lh[:, 0:E]))
                    held(dve, dve_passed)
                    link(nc.vector.max_index(topi[:], top[:], lh[:, 0:E]))
                    link(nc.vector.tensor_copy(topf[:], topi[:, 0:2]))
                    link(nc.vector.tensor_tensor(dtop[:], top[:, 1:2], top[:, 0:1], ALU.subtract))
                    dve.wait_ge(gates_tanh, t + 1)
                    link(nc.vector.tensor_scalar(topw[:], topt[:], 0.5, 0.5, ALU.mult, ALU.add))
                    link(nc.vector.tensor_scalar(wexp[:, 0], iota[:], topf[:, 0:1], topw[:, 0:1], ALU.is_equal, ALU.mult))
                    link(nc.vector.tensor_scalar(wexp[:, 1], iota[:], topf[:, 1:2], topw[:, 1:2], ALU.is_equal, ALU.mult))
                    link(nc.vector.tensor_tensor(wexp[:, 0], wexp[:, 0], wexp[:, 1], ALU.add))
                    nc.vector.tensor_tensor(hw[:].rearrange("p (e r) -> p e r", r=R), lh[:, E:].rearrange("p (e r) -> p e r", r=R),
                                            wexp[:, 0].unsqueeze(2).to_broadcast([128, E, R]), ALU.mult).then_inc(hw_ready, 1)
                    dve.wait_ge(affine, t + 1)
                    bk, n = turn.count(("gate", j, 1))
                    dve.wait_ge(w_freed[bk], n + 1)
                    bk, n = turn.count(("gate", j, 0))
                    dve.wait_ge(w_freed[bk], n + 1)
                    o = ot[:, j % 2]
                    nc.vector.scalar_tensor_tensor(out=o, in0=gl[:], scalar=1.0, in1=o, op0=ALU.add, op1=ALU.mult).then_inc(og_done, 1)

                for j in range(NT):
                    if attention:
                        attend(j)
                    if tiles_:
                        tile(j)
                    if attention:
                        join(j)
                if tiles_:
                    link = linker(xn2_chain, XN2_OPS * (b + 1))
                    dve.wait_ge(x1_done, NT * (b + 2))
                    for t in range(NT):
                        link(nc.vector.bn_stats(bst2[:, t, :], x1[:, t, :]))
                        held(dve, dve_passed)
                        link(nc.vector.bn_aggr(mv2[:, t, :], bst2[:, t, :]))
                    link(nc.vector.tensor_scalar(var2[:], mv2[:, :, 1], EPS, None, ALU.add))
                    rsqrt_ops(nc, rs2[:], var2[:], rstmp2[:], link)
                    for t in range(NT):
                        nc.vector.tensor_scalar(xn2[:, t, :], x1[:, t, :], mv2[:, t, 0:1], rs2[:, t:t + 1], ALU.subtract, ALU.mult).then_inc(xn2_ready, 1)
                    for t in range(NT // 2):
                        bank, freed = filled("v", t)
                        nc.vector.tensor_tensor(v[:, 2 * t:2 * t + 2, :, 0:D1], bank[:].rearrange("p (t h d) -> p t h d", t=2, d=D1),
                                                bv[:].rearrange("p (h d) -> p h d", d=D1).unsqueeze(1).to_broadcast([128, 2, H1, D1]),
                                                ALU.add).then_inc(freed, 1)
                    for t in range(NT // 2):
                        bank, freed = filled("rest", t)
                        nc.vector.tensor_tensor(rest[:, 2 * t:2 * t + 2].rearrange("p t n -> p (t n)"), bank[:],
                                                x1[:, 2 * t:2 * t + 2].rearrange("p t n -> p (t n)"), ALU.add).then_inc(freed, 1)
            turns(dve, body)


def _heads32(w, fill=0.0):
    out = np.zeros(w.shape[:-1] + (HG, 4, 32), w.dtype)
    out[..., 0:D1] = w.reshape(w.shape[:-1] + (HG, 4, D1))
    out[..., D1] = fill
    return out.reshape(w.shape[:-1] + (HG, 128))


_LAID = {
    "wqkv": lambda i: np.concatenate([i["L0_attn_Wq"].T, i["L0_attn_Wk"].T, i["L0_attn_Wv"].T], axis=1),
    "wa": lambda i: i["L0_attn_Wa"].T,
    "wbeta": lambda i: i["L0_attn_Wb"].T,
    "conv_w": lambda i: np.concatenate([i["L0_attn_qcw"], i["L0_attn_kcw"], i["L0_attn_vcw"]])
                          .reshape(MT, 128, TAPS).transpose(1, 0, 2),
    "conv_b": lambda i: np.concatenate([i["L0_attn_qcb"], i["L0_attn_kcb"], i["L0_attn_vcb"]]).reshape(MT, 128).T,
    "wg": lambda i: i["L0_attn_Wg"].T,
    "wsm": lambda i: np.concatenate([i["L0_ffn_gate_W"].T, i["L0_ffn_lora_down"].reshape(ER, HID).T], axis=1),
    "wbase": lambda i: i["L0_ffn_W_base"].T,
    "wo": lambda i: i["L0_attn_Wo"].T,
    "lup": lambda i: i["L0_ffn_lora_up"].transpose(0, 2, 1).reshape(ER, HID),
    "wqk": lambda i: np.concatenate([_heads32(i["L1_attn_w_qkv"][:, 0:256]), _heads32(i["L1_attn_w_qkv"][:, 256:512])], axis=1),
    "bqk": lambda i: np.concatenate([_heads32(i["L1_attn_b_qkv"][0:256]), _heads32(i["L1_attn_b_qkv"][256:512], 1.0)], axis=0).T,
    "wv": lambda i: i["L1_attn_w_qkv"][:, 512:768],
    "bv": lambda i: i["L1_attn_b_qkv"][512:768],
    "aT": lambda i: i["L1_ffn_a"].T,
}
_AS_IS = ["L0_attn_x", "L0_attn_ba", "L0_attn_bb", "L0_ffn_gate_b", "L0_ffn_b_base", "L0_attn_ln_w", "L0_attn_ln_b",
          "L1_attn_w_out", "L1_attn_b_out", "L1_ffn_bias", "L1_ffn_kernel", "L1_ffn_b"]


def program(nc, ins, out):
    o_dram = nc.dram_tensor("o_dram", [T, B, H, DV], f32).ap()
    layer0_recurrence(nc, ins, o_dram)
    layer0_end_and_layer1(nc, ins, o_dram, out)


def kernel(**inputs):
    import concourse.bacc as bacc
    from concourse.bass_utils import run_bass_kernel_spmd

    arrays = {name: np.asarray(inputs[name]) for name in inputs}
    arrays = {name: arrays[name] for name in _AS_IS} | {name: lay(arrays) for name, lay in _LAID.items()}
    arrays = {name: np.ascontiguousarray(a) for name, a in arrays.items()}
    nc = bacc.Bacc("TRN2", target_bir_lowering=False, num_devices=1)
    ins = {name: nc.dram_tensor(f"in_{name}", a.shape, f32, kind="ExternalInput").ap() for name, a in arrays.items()}
    out = nc.dram_tensor("out", [B, T, HID], f32, kind="ExternalOutput").ap()
    program(nc, ins, out)
    result = run_bass_kernel_spmd(nc, [{f"in_{name}": a for name, a in arrays.items()}], core_ids=[0])
    return result.results[0]["out"]
```

```python
import numpy as np
import concourse.bass as bass
from concourse import mybir
from contextlib import ExitStack

B, T, HID = 16, 512, 256
H, DK, DV, TAPS = 16, 64, 64, 4
HD = H * DV
C = 16
GB = 8
GROUPS = B // GB
P = GB * C
STEPS = (T // C) * GROUPS
HP = H // 2
MT = 3 * HD // 128
ROW = DV + C
SLOT = DV + 2 * C
E, R = 10, 4
ER = E * R
EPS = 1e-5
F1_USES, F2_USES = 10, 4
F_USES = F1_USES + F2_USES
F_BANKS = 2
CONV_OPS = MT * (TAPS - 1)
SHARED_FROM = 11
SHARES = [(r, t) for r in range(SHARED_FROM, C) for t in range(r, C)]
SOLVE_OPS = 2 + C + 3 * (C - 1) + 1
ADDS_BEFORE, ADDS_PER_ROW = 2, 2
TAP_GROUPS = 6 * (TAPS - 1)
DECAY_OPS = C
POOL_OPS = DECAY_OPS + 2 + 3 * SHARED_FROM + 2 * (C - SHARED_FROM)
RSQRT_OPS = 14

H1, D1 = 16, 16
NT = T // 128
PARTS = 3
PAIRS = [(q, k) for q in range(PARTS) for k in range(PARTS - q)]
ROWS = D1 * len(PAIRS)
QK_TILES = 2 * H1 // 8
RSQRT_MAGIC = float(0x5F3759DF)
ROUND = 1.5 * 2.0 ** 23

f32 = mybir.dt.float32
bf16 = mybir.dt.bfloat16
i32 = mybir.dt.int32
u32 = mybir.dt.uint32
ALU = mybir.AluOpType
ACT = mybir.ActivationFunctionType
AX = mybir.AxisListType


def due(value):
    return not isinstance(value, int) or value > 0


def held(engine, passed):
    engine.sem_inc(passed, 1)


def rsqrt_ops(nc, y, v, t, link):
    link(nc.vector.tensor_scalar(t.bitcast(i32), v.bitcast(i32), 1, None, ALU.logical_shift_right))
    link(nc.vector.tensor_scalar(y.bitcast(i32), t.bitcast(i32), -1.0, RSQRT_MAGIC, ALU.mult, ALU.add))
    for _ in range(3):
        link(nc.vector.tensor_tensor(t, y, y, ALU.mult))
        link(nc.vector.tensor_tensor(t, t, v, ALU.mult))
        link(nc.vector.tensor_scalar(t, t, -0.5, 1.5, ALU.mult, ALU.add))
        link(nc.vector.tensor_tensor(y, y, t, ALU.mult))


def dma_of(sems, n, g, ahead, each=16):
    return sems[(g + ahead) % GROUPS], each * (n + (g + ahead) // GROUPS + 1)


def slot_loop(engine, slot, first, last, loop):
    for s in range(first, loop[0]):
        slot(s, (s - s % 2) // 2, s % 2, s, s)
    with engine.Fori(0, (loop[1] - loop[0] + 1) // 2) as i:
        for g in range(2):
            slot(2 * i + (loop[0] + g), i + loop[0] // 2, g, loop[0], loop[1])
    for s in range(loop[1] + 1, last + 1):
        slot(s, (s - s % 2) // 2, s % 2, s, s)


def layer0_recurrence(nc, ins, o_dram):
    def dram(name, shape):
        return nc.dram_tensor(name, shape, f32).ap()

    prod_dram = [dram(f"prod_dram{g}", [GB * 4, P, ROW]) for g in range(GROUPS)]
    v_dram = [dram(f"v_dram{g}", [C, GB, H, DV]) for g in range(GROUPS)]
    a_dram = [dram(f"a_dram{g}", [C, GB, H, DV]) for g in range(GROUPS)]
    beta_dram = [dram(f"beta_dram{g}", [GB, H, C]) for g in range(GROUPS)]
    upd_dram = [dram(f"upd_dram{g}", [GB, H, C, DV]) for g in range(GROUPS)]
    decay_dram = [dram(f"decay_dram{g}", [GB * H, DV]) for g in range(GROUPS)]
    x = ins["L0_attn_x"]

    with ExitStack() as ctx:
        def sb(name, shape, dt=f32):
            return ctx.enter_context(nc.sbuf_tensor(name, shape, dt))

        def ps(name, shape):
            return ctx.enter_context(nc.psum_tensor(name, shape, f32))

        def sem(name):
            return ctx.enter_context(nc.semaphore(name))

        ident = sb("ident", [128, 128])
        ones = sb("ones", [1, 128])
        wqkv = sb("wqkv", [128, 2, 3 * HD])
        wa = sb("wa", [128, 2, HD])
        wbeta = sb("wbeta", [128, 2, H])
        ba = sb("ba", [1, HD])
        bb = sb("bb", [H, 1])
        conv_w = sb("conv_w", [128, MT, TAPS])
        conv_b = sb("conv_b", [128, MT])
        xt = sb("xt", [P, HID])
        xn = sb("xn", [P, HID])
        xnT = sb("xnT", [128, 2, 2, P])
        y = sb("y", [128, MT, GB, TAPS - 1 + C])
        halo = sb("halo", [128, 2, MT, GB, TAPS - 1])
        z = sb("z", [128, MT, P])
        sg = sb("sg", [128, 2, HP, P])
        bt = sb("bt", [H, P])
        vt, at = (sg[:, i].rearrange("p h t -> p (h t)") for i in range(2))
        st = [sb(f"st{g}", [128, GB, HP, SLOT]) for g in range(GROUPS)]
        decay_or_prod = sb("decay_or_prod", [128, GB * HP * DV])
        db = decay_or_prod[:].rearrange("p (m i) -> p m i", i=DV)
        prod = decay_or_prod[:, 0:GB * 4 * ROW].rearrange("p (b c) -> p b c", b=GB)
        kp = sb("kp", [128, C, ROW])
        qp = sb("qp", [128, 2, C, ROW])
        vb = sb("vb", [128, 2, C, DV])
        ab = sb("ab", [128, 2, C, DV])
        nb = sb("nb", [128, 2, C])
        eb = sb("eb", [128, C, DV])
        acb = sb("acb", [128, DV])
        t2 = sb("t2", [128, C - 1, DV])
        pt2 = sb("pt2", [128, C, DV])
        share = sb("share", [128, len(SHARES), DV])
        kt = sb("kt", [P, 2, HD])
        xd = sb("xd", [P, H, 2, DV])
        norm_work = sb("norm_work", [P, 11])
        bst, mv, var, rs, rstmp = (norm_work[:, a:b] for a, b in ((0, 6), (6, 8), (8, 9), (9, 10), (10, 11)))

        p_bank = [ps(f"p_bank{i}", [128, 512]) for i in range(2)]
        f_bank = [ps(f"f_bank{i}", [128, 512]) for i in range(F_BANKS)]
        d_bank = [ps(f"d_bank{i}", [128, 512]) for i in range(2)]

        consts_in = sem("consts_in")
        ident_done = sem("ident_done")
        init_done = sem("init_done")
        x_in = [sem(f"x_in{g}") for g in range(GROUPS)]
        xn_ready, norm_chain = sem("xn_ready"), sem("norm_chain")
        f_filled, f_freed = sem("f_filled"), sem("f_freed")
        p_filled, p_freed = sem("p_filled"), sem("p_freed")
        d_filled, d_freed = sem("d_filled"), sem("d_freed")
        keys_placed = sem("keys_placed")
        conv_chain, sg_ready, silu_done = sem("conv_chain"), sem("sg_ready"), sem("silu_done")
        halo_done, bneg_done = sem("halo_done"), sem("bneg_done")
        a_wr, beta_wr, v_wr, p_wr, qp_in, kp_in, vb_in, ab_in, nb_in, upd_wr, xd_in, dec_wr, db_in, o_wr = (
            [sem(f"{name}{g}") for g in range(GROUPS)] for name in
            ("a_wr", "beta_wr", "v_wr", "p_wr", "qp_in", "kp_in", "vb_in", "ab_in", "nb_in", "upd_wr", "xd_in",
             "dec_wr", "db_in", "o_wr"))
        solve_chain, pool_chain = sem("solve_chain"), sem("pool_chain")
        decayed, shares_done = sem("decayed"), sem("shares_done")
        sp_passed, pool_passed, pe_passed, dve_passed = map(sem, ("sp_passed", "pool_passed", "pe_passed", "dve_passed"))

        FIRST, LOOP, LAST = -2, (4, STEPS - 5), STEPS
        block = ctx.enter_context(nc.Block())

        def valid(lo, hi):
            return 0 <= lo and hi < STEPS

        def updates(lo, hi):
            return 0 <= lo and hi < STEPS - GROUPS

        @block.sync
        def _(sp):
            for tile, src in (
                (wqkv[:], ins["wqkv"].rearrange("(k p) n -> p k n", p=128)),
                (wa[:], ins["wa"].rearrange("(k p) n -> p k n", p=128)),
                (wbeta[:], ins["wbeta"].rearrange("(k p) n -> p k n", p=128)),
                (ba[:], ins["L0_attn_ba"].rearrange("(a n) -> a n", a=1)),
                (bb[:], ins["L0_attn_bb"].rearrange("(n a) -> n a", a=1)),
                (conv_w[:], ins["conv_w"]),
                (conv_b[:], ins["conv_b"]),
            ):
                sp.dma_start(tile, src).then_inc(consts_in, 16)

            def load_x(n, g):
                src = x[GB * g:GB * g + GB].rearrange("b (n t) c -> n b t c", t=C)
                sp.dma_start(xt[:], src[bass.ds(n, 1)]).then_inc(x_in[g], 16)

            def slot(s, n, g, lo, hi):
                o = 1 - g
                if valid(lo + 2, hi + 2):
                    if due(s + 2):
                        sp.wait_ge(xn_ready, s + 2)
                    held(sp, sp_passed)
                    load_x(n + 1, g)
                if updates(lo - 1, hi - 1):
                    t = s - 1
                    sp.wait_ge(*dma_of(p_wr, n, g, 0))
                    held(sp, sp_passed)
                    sp.wait_ge(*dma_of(dec_wr, n, g, -1))
                    held(sp, sp_passed)
                    for par in range(2):
                        src = decay_dram[o].rearrange("(m two) i -> two m i", two=2)[par:par + 1]
                        sp.dma_start(db[64 * par:64 * par + 64], src.to_broadcast([64, GB * HP, DV])).then_inc(db_in[o], 16)
                    sp.wait_ge(solve_chain, SOLVE_OPS * (t + 1))
                    held(sp, sp_passed)
                    if due(dma_of(xd_in, n, g, -3, 16 * GB)[1]):
                        sp.wait_ge(*dma_of(xd_in, n, g, -3, 16 * GB))
                        held(sp, sp_passed)
                    sp.dma_start(upd_dram[o].rearrange("b h t i -> (b h) (t i)"), eb[:]).then_inc(upd_wr[o], 16)
                    sp.wait_ge(*dma_of(upd_wr, n, g, -1))
                    held(sp, sp_passed)
                    if due(8 * t):
                        sp.wait_ge(d_filled, 8 * t)
                        held(sp, sp_passed)
                    for b in range(GB):
                        sp.dma_start(xd[C * b:C * b + C, :, b % 2, :],
                                     upd_dram[o][b].rearrange("h t i -> t h i")).then_inc(xd_in[o], 16)
                if valid(lo, hi):
                    sp.wait_ge(*dma_of(p_wr, n, g, 0))
                    held(sp, sp_passed)
                    if due(SOLVE_OPS * s):
                        sp.wait_ge(solve_chain, SOLVE_OPS * s)
                        held(sp, sp_passed)
                    src = prod_dram[g].rearrange("m (h k r) c -> (m h) k r c", h=4, k=2)
                    sp.dma_start(kp[:], src[:, 0]).then_inc(kp_in[g], 16)
                    if due(dma_of(o_wr, n, g, -2)[1]):
                        sp.wait_ge(*dma_of(o_wr, n, g, -2))
                        held(sp, sp_passed)
                    sp.dma_start(qp[:, g], src[:, 1]).then_inc(qp_in[g], 16)
                if valid(lo + 1, hi + 1):
                    t = s + 1
                    if due(POOL_OPS * (t - 1)):
                        sp.wait_ge(pool_chain, POOL_OPS * (t - 1))
                        held(sp, sp_passed)
                    sp.wait_ge(*dma_of(v_wr, n, g, 1))
                    held(sp, sp_passed)
                    sp.dma_start(vb[:, o], v_dram[o].rearrange("t b h i -> (b h) t i")).then_inc(vb_in[o], 16)
                    sp.wait_ge(*dma_of(a_wr, n, g, 1))
                    held(sp, sp_passed)
                    sp.dma_start(ab[:, o], a_dram[o].rearrange("t b h i -> (b h) t i")).then_inc(ab_in[o], 16)
                    sp.wait_ge(*dma_of(beta_wr, n, g, 1))
                    held(sp, sp_passed)
                    sp.dma_start(nb[:, o], beta_dram[o].rearrange("b h t -> (b h) t")).then_inc(nb_in[o], 16)
                if updates(lo, hi):
                    sp.wait_ge(pool_chain, POOL_OPS * s + DECAY_OPS)
                    held(sp, sp_passed)
                    if due(dma_of(db_in, n, g, -2, 32)[1]):
                        sp.wait_ge(*dma_of(db_in, n, g, -2, 32))
                        held(sp, sp_passed)
                    sp.dma_start(decay_dram[g], acb[:]).then_inc(dec_wr[g], 16)
                if valid(lo - 1, hi - 1):
                    t = s - 1
                    sp.wait_ge(pool_chain, POOL_OPS * (t + 1))
                    held(sp, sp_passed)
                    dst = o_dram.rearrange("(n t) b h i -> n t b h i", t=C)[:, :, GB * o:GB * o + GB]
                    sp.dma_start(dst[bass.ds(n - 1 + g, 1)].rearrange("o t b h i -> (o b h) t i"), qp[:, o, :, 0:DV]).then_inc(o_wr[o], 16)
                if lo == LAST:
                    for g in range(GROUPS):
                        sp.wait_ge(o_wr[g], 16 * STEPS // GROUPS)

            slot_loop(sp, slot, FIRST, LAST, LOOP)

        @block.gpsimd
        def _(pool):
            nc.gpsimd.memset(ident[:], 0.0).then_inc(ident_done, 1)
            pool.wait_ge(ident_done, 1)
            nc.gpsimd.affine_select(out=ident[:], in_=ident[:], compare_op=ALU.not_equal, fill=1.0, base=0,
                                    pattern=[[-1, 128]], channel_multiplier=1).then_inc(ident_done, 1)
            pool.wait_ge(init_done, 1)

            def slot(s, n, g, lo, hi):
                if not valid(lo, hi):
                    return
                base, made = POOL_OPS * s, [0]

                def link(ins, back=0):
                    made[0] += 1
                    ins.then_inc(pool_chain, 1)
                    pool.wait_ge(pool_chain, base + made[0] - back)

                pool.wait_ge(*dma_of(ab_in, n, g, 0))
                pool.wait_ge(*dma_of(nb_in, n, g, 0))
                if updates(lo - 1, hi - 1):
                    pool.wait_ge(*dma_of(upd_wr, n, g, -1))
                if due(SOLVE_OPS * s):
                    pool.wait_ge(solve_chain, SOLVE_OPS * s)
                held(pool, pool_passed)
                link(nc.gpsimd.tensor_copy(eb[:, C - 2, :], ab[:, g, C - 1, :]))
                for r in range(C - 3, -1, -1):
                    link(nc.gpsimd.tensor_tensor(eb[:, r, :], eb[:, r + 1, :], ab[:, g, r + 1, :], ALU.mult))
                if updates(lo - 1, hi - 1):
                    pool.wait_ge(*dma_of(dec_wr, n, g, -1))
                link(nc.gpsimd.tensor_tensor(acb[:], eb[:, 0, :], ab[:, g, 0, :], ALU.mult))
                link(nc.gpsimd.tensor_tensor(eb[:, 0:C - 1], eb[:, 0:C - 1],
                                             nb[:, g, 0:C - 1].unsqueeze(2).to_broadcast([128, C - 1, DV]), ALU.mult))
                held(pool, pool_passed)
                link(nc.gpsimd.tensor_copy(eb[:, C - 1, :], nb[:, g, C - 1:C].to_broadcast([128, DV])))
                pool.wait_ge(*dma_of(qp_in, n, g, 0))
                for r in range(C):
                    q = qp[:, g, r:C, 0:DV]
                    w = C - r
                    shared = r >= SHARED_FROM
                    link(nc.gpsimd.tensor_tensor(q, q, ab[:, g, r:r + 1, :].to_broadcast([128, w, DV]), ALU.mult), 0 if shared else 1)
                    if shared:
                        at_ = SHARES.index((r, r))
                        pool.wait_ge(shares_done, (C - SHARED_FROM) * s + r - SHARED_FROM + 1)
                        link(nc.gpsimd.tensor_tensor(q, q, share[:, at_:at_ + w], ALU.add))
                        continue
                    pool.wait_ge(solve_chain, SOLVE_OPS * s + 2 + 4 * r + 1)
                    link(nc.gpsimd.tensor_tensor(
                        pt2[:, 0:w], qp[:, g, r:C, DV + r:DV + r + 1].to_broadcast([128, w, DV]),
                        vb[:, g, r:r + 1, :].to_broadcast([128, w, DV]), ALU.mult))
                    link(nc.gpsimd.tensor_tensor(q, q, pt2[:, 0:w], ALU.add))
                assert made[0] == POOL_OPS

            slot_loop(pool, slot, FIRST, LAST, LOOP)

        @block.tensor
        def _(pe):
            pe.wait_ge(consts_in, 16 * 7)
            pe.wait_ge(ident_done, 2)
            pe.wait_ge(init_done, 1)

            def use(s, k):
                if due(F_USES * s + k - F_BANKS + 1):
                    pe.wait_ge(f_freed, F_USES * s + k - F_BANKS + 1)
                return f_bank[k % F_BANKS]

            def update(s, n, g):
                pe.wait_ge(f_freed, F_USES * s + F1_USES + 2)
                pe.wait_ge(*dma_of(xd_in, n, g, 0, 16 * GB))
                for u in range(8):
                    q, hh = u // 2, u % 2
                    if due(8 * s + u - 1):
                        pe.wait_ge(d_freed, 8 * s + u - 1)
                    for k in range(4):
                        for par in range(2):
                            h = 2 * (4 * hh + k) + par
                            mm = nc.tensor.matmul(d_bank[u % 2][64 * par:64 * par + 64, 128 * k:128 * k + 128],
                                                  kt[32 * q:32 * q + 32, g, DK * h:DK * h + DK],
                                                  xd[32 * q:32 * q + 32, h, :, :], start=True, stop=True)
                    mm.then_inc(d_filled, 1)

            def front2(s, n, g):
                for j in range(4):
                    bank = use(s, F1_USES + j)
                    pe.wait_ge(silu_done, 3 * s + 2 + j // 2)
                    for i in range(4):
                        mm = nc.tensor.transpose(bank[:, 128 * i:128 * i + 128], z[:, HP + 4 * j + i, :], ident[:])
                    mm.then_inc(f_filled, 1)

            def products(s, n, g):
                if due(8 * (s - 1)):
                    pe.wait_ge(d_freed, 8 * (s - 1))
                pe.wait_ge(silu_done, 3 * s + 1)
                pe.wait_ge(keys_placed, s + 1)
                for b in range(GB):
                    if due(8 * s + b - 1):
                        pe.wait_ge(p_freed, 8 * s + b - 1)
                    held(pe, pe_passed)
                    for hq in range(4):
                        for hpo in range(2):
                            for par in range(2):
                                at_ = 32 * (2 * hpo + par)
                                slot_ = st[g][64 * par:64 * par + 64, b, 2 * hq + hpo, :]
                                mm = nc.tensor.matmul(p_bank[b % 2][at_:at_ + 32, ROW * hq:ROW * hq + ROW],
                                                      slot_[:, DV:DV + 2 * C], slot_[:, 0:ROW], start=True, stop=True)
                    mm.then_inc(p_filled, 1)

            def front1(s, n, g):
                bank = use(s, 0)
                pe.wait_ge(xn_ready, s + 1)
                for k in range(2):
                    mm = nc.tensor.transpose(bank[:, 128 * k:128 * k + 128], xn[:, 128 * k:128 * k + 128], ident[:])
                mm.then_inc(f_filled, 1)
                pe.wait_ge(f_freed, F_USES * s + 1)
                for j in range(6):
                    bank = use(s, 1 + j)
                    for i in range(4):
                        m = 4 * j + i
                        for k in range(2):
                            mm = nc.tensor.matmul(bank[:, 128 * i:128 * i + 128], wqkv[:, k, 128 * m:128 * m + 128],
                                                  xnT[:, g, k, :], start=k == 0, stop=k == 1)
                    mm.then_inc(f_filled, 1)
                for j in range(2):
                    bank = use(s, 7 + j)
                    for k in range(2):
                        nc.tensor.matmul(bank[:], xnT[:, g, k, :], wa[:, k, 512 * j:512 * j + 512], start=k == 0, stop=False)
                    nc.tensor.matmul(bank[:], ones[:], ba[:, 512 * j:512 * j + 512], start=False, stop=True).then_inc(f_filled, 1)
                bank = use(s, 9)
                for k in range(2):
                    mm = nc.tensor.matmul(bank[0:H, 0:P], wbeta[:, k, :], xnT[:, g, k, :], start=k == 0, stop=k == 1)
                mm.then_inc(f_filled, 1)

            def slot(s, n, g, lo, hi):
                if updates(lo - 1, hi - 1):
                    update(s - 1, n - 1 + g, 1 - g)
                if valid(lo + 1, hi + 1):
                    front2(s + 1, n + g, 1 - g)
                    products(s + 1, n + g, 1 - g)
                if valid(lo + 2, hi + 2):
                    front1(s + 2, n + 1, g)

            slot_loop(pe, slot, FIRST, LAST, LOOP)

        @block.scalar
        def _(act):
            act.wait_ge(init_done, 1)

            def filled(s, k):
                act.wait_ge(f_filled, F_USES * s + k + 1)
                return f_bank[k % F_BANKS]

            def sigmoids(s, n, g):
                if due(dma_of(v_wr, n, g, -1)[1]):
                    act.wait_ge(*dma_of(v_wr, n, g, -1))
                act.wait_ge(*dma_of(a_wr, n, g, 0))
                for j in range(3):
                    act.wait_ge(conv_chain, CONV_OPS * s + CONV_OPS // 3 * (j + 1))
                    if due(3 * s + j - 1):
                        act.wait_ge(silu_done, 3 * s + j - 1)
                    nc.scalar.activation(sg[:, j % 2], z[:, HP * j:HP * j + HP, :], ACT.Sigmoid,
                                         scale=float(DK) ** 0.5 if j == 1 else 1.0).then_inc(sg_ready, 1)

            def front2(s, n, g):
                act.wait_ge(silu_done, 3 * s + 2)
                if due(8 * (s - 1)):
                    act.wait_ge(p_filled, 8 * (s - 1))
                nc.scalar.activation(st[g][:, :, :, DV:DV + C], z[:, HP:2 * HP, :].rearrange("p h (b t) -> p b h t", b=GB),
                                     ACT.Copy).then_inc(keys_placed, 1)
                if due(8 * (s - 1)):
                    act.wait_ge(d_filled, 8 * (s - 1))
                for j in range(4):
                    bank = filled(s, F1_USES + j)
                    dst = kt[:, g] if j < 2 else vt
                    nc.scalar.activation(dst[:, 512 * (j % 2):512 * (j % 2) + 512], bank[:], ACT.Copy).then_inc(f_freed, 1)
                act.wait_ge(f_freed, F_USES * (s + 1))
                if due(dma_of(vb_in, n, g, -2)[1]):
                    act.wait_ge(*dma_of(vb_in, n, g, -2))
                act.dma_start(v_dram[g].rearrange("t b h i -> b t (h i)"), vt).then_inc(v_wr[g], 16)

            def shares(s, g, tokens):
                for r in tokens:
                    act.wait_ge(solve_chain, SOLVE_OPS * s + 2 + 4 * r + 1)
                    if r == SHARED_FROM and due(POOL_OPS * s):
                        act.wait_ge(pool_chain, POOL_OPS * s)
                    for t in range(r, C):
                        last = nc.scalar.activation(share[:, SHARES.index((r, t))], vb[:, g, r, :], ACT.Copy,
                                                    scale=qp[:, g, t, DV + r:DV + r + 1])
                    last.then_inc(shares_done, 1)

            def products(s, n, g):
                if due(dma_of(p_wr, n, g, -1)[1]):
                    act.wait_ge(*dma_of(p_wr, n, g, -1))
                for b in range(GB):
                    act.wait_ge(p_filled, 8 * s + b + 1)
                    nc.scalar.activation(prod[:, b, :], p_bank[b % 2][:, 0:4 * ROW], ACT.Copy).then_inc(p_freed, 1)
                act.wait_ge(p_freed, 8 * s + 8)
                if due(dma_of(qp_in, n, g, -2)[1]):
                    act.wait_ge(*dma_of(qp_in, n, g, -2))
                if due(dma_of(kp_in, n, g, -2)[1]):
                    act.wait_ge(*dma_of(kp_in, n, g, -2))
                act.dma_start(prod_dram[g].rearrange("m p c -> p m c"), prod.rearrange("p b (q c) -> p (b q) c", c=ROW)).then_inc(p_wr[g], 16)

            def front1(s, n, g):
                if due(3 * s):
                    act.wait_ge(silu_done, 3 * s)
                if due(F_USES * s):
                    act.wait_ge(f_filled, F_USES * s)
                nc.scalar.activation(y[:, :, :, 0:TAPS - 1], halo[:, g], ACT.Copy).then_inc(halo_done, 1)
                act.wait_ge(halo_done, s + 1)
                bank = filled(s, 0)
                nc.scalar.activation(xnT[:, g].rearrange("p k t -> p (k t)"), bank[:, 0:2 * P], ACT.Copy).then_inc(f_freed, 1)
                for j in range(6):
                    bank = filled(s, 1 + j)
                    now = bank[:].rearrange("p (m b t) -> p m b t", m=4, b=GB)
                    for i in range(4):
                        m = 4 * j + i
                        nc.scalar.activation(z[:, m, :], bank[:, 128 * i:128 * i + 128], ACT.Identity,
                                             bias=conv_b[:, m:m + 1], scale=conv_w[:, m, TAPS - 1:TAPS])
                    nc.scalar.activation(halo[:, g, 4 * j:4 * j + 4], now[:, :, :, C - TAPS + 1:], ACT.Copy)
                    nc.scalar.activation(y[:, 4 * j:4 * j + 4, :, TAPS - 1:], now, ACT.Copy).then_inc(f_freed, 1)
                for j in range(2):
                    bank = filled(s, 7 + j)
                    nc.scalar.activation(at[:, 512 * j:512 * j + 512], bank[:], ACT.Sigmoid).then_inc(f_freed, 1)
                act.wait_ge(f_freed, F_USES * s + 9)
                if due(dma_of(ab_in, n, g, -2)[1]):
                    act.wait_ge(*dma_of(ab_in, n, g, -2))
                act.dma_start(a_dram[g].rearrange("t b h i -> b t (h i)"), at).then_inc(a_wr[g], 16)
                bank = filled(s, 9)
                if due(dma_of(beta_wr, n, g, -1)[1]):
                    act.wait_ge(*dma_of(beta_wr, n, g, -1))
                nc.scalar.activation(bt[:], bank[0:H, 0:P], ACT.Sigmoid, bias=bb[:]).then_inc(f_freed, 1)
                act.wait_ge(f_freed, F_USES * s + 10)
                nc.scalar.activation(bt[:], bt[:], ACT.Copy, scale=-1.0).then_inc(bneg_done, 1)
                act.wait_ge(bneg_done, s + 1)
                if due(dma_of(nb_in, n, g, -2)[1]):
                    act.wait_ge(*dma_of(nb_in, n, g, -2))
                act.dma_start(beta_dram[g].rearrange("b h t -> h b t"), bt[:].rearrange("h (b t) -> h b t", b=GB)).then_inc(beta_wr[g], 16)

            def slot(s, n, g, lo, hi):
                if valid(lo + 1, hi + 1):
                    sigmoids(s + 1, n + g, 1 - g)
                    front2(s + 1, n + g, 1 - g)
                    products(s + 1, n + g, 1 - g)
                if valid(lo + 2, hi + 2):
                    front1(s + 2, n + 1, g)
                if valid(lo, hi):
                    shares(s, g, range(SHARED_FROM, C))

            slot_loop(act, slot, FIRST, LAST, LOOP)

        @block.vector
        def _(dve):
            for g in range(2):
                nc.vector.memset(st[g][:, :, :, 0:DV], 0.0)
            nc.vector.memset(xd[:], 0.0)
            nc.vector.memset(ones[:], 1.0)
            nc.vector.memset(halo[:], 0.0)
            dve.wait_ge(consts_in, 16 * 7)
            nc.vector.tensor_scalar(conv_w[:, HP:2 * HP, :], conv_w[:, HP:2 * HP, :], float(DK) ** -0.5, None, ALU.mult)
            nc.vector.tensor_scalar(conv_b[:, HP:2 * HP], conv_b[:, HP:2 * HP], float(DK) ** -0.5, None, ALU.mult).then_inc(init_done, 1)
            dve.wait_ge(init_done, 1)

            def conv(s, k):
                j, tap = k // (TAPS - 1), k % (TAPS - 1)
                dve.wait_ge(f_freed, F_USES * s + j + 2)
                for i in range(4):
                    m = 4 * j + i
                    if tap:
                        dve.wait_ge(conv_chain, CONV_OPS * s + 4 * k + i - 3)
                    zz = z[:, m, :].rearrange("p (b t) -> p b t", b=GB)
                    nc.vector.scalar_tensor_tensor(
                        out=zz, in0=y[:, m, :, tap:tap + C], scalar=conv_w[:, m, tap:tap + 1], in1=zz,
                        op0=ALU.mult, op1=ALU.add).then_inc(conv_chain, 1)

            def silu(s, g, j):
                if j == 0 and due(8 * (s - 1)):
                    dve.wait_ge(p_filled, 8 * (s - 1))
                dve.wait_ge(sg_ready, 3 * s + j + 1)
                v = z[:, HP * j:HP * j + HP, :]
                if j == 0:
                    nc.vector.tensor_tensor(st[g][:, :, :, DV + C:DV + 2 * C], v.rearrange("p h (b t) -> p b h t", b=GB),
                                            sg[:, 0].rearrange("p h (b t) -> p b h t", b=GB),
                                            ALU.mult).then_inc(silu_done, 1)
                else:
                    nc.vector.tensor_tensor(v, v, sg[:, j % 2], ALU.mult).then_inc(silu_done, 1)

            def decay(s, n, g):
                dve.wait_ge(*dma_of(db_in, n, g, 0, 32))
                dve.wait_ge(p_filled, 8 * (s + 1))
                sv = st[g][:, :, :, 0:DV]
                nc.vector.tensor_tensor(sv.rearrange("p b h i -> p (b h) i"), sv.rearrange("p b h i -> p (b h) i"), db[:],
                                        ALU.mult).then_inc(decayed, 1)

            def state(s, g, u):
                q, hh = u // 2, u % 2
                if u == 0:
                    dve.wait_ge(decayed, s + 1)
                dve.wait_ge(d_filled, 8 * s + u + 1)
                part = st[g][:, 2 * q:2 * q + 2, 4 * hh:4 * hh + 4, 0:DV]
                nc.vector.tensor_tensor(part, d_bank[u % 2][:].rearrange("p (h b i) -> p b h i", h=4, b=2), part,
                                        ALU.add).then_inc(d_freed, 1)

            def norm(s, n, g, meanwhile):
                base, made = (3 + RSQRT_OPS) * s, [0]

                def link(ins):
                    made[0] += 1
                    ins.then_inc(norm_chain, 1)
                    meanwhile()
                    dve.wait_ge(norm_chain, base + made[0])

                dve.wait_ge(x_in[g], 16 * (n + 1))
                link(nc.vector.bn_stats(bst[:], xt[:]))
                held(dve, dve_passed)
                link(nc.vector.bn_aggr(mv[:], bst[:]))
                link(nc.vector.tensor_scalar(var[:], mv[:, 1:2], EPS, None, ALU.add))
                rsqrt_ops(nc, rs[:], var[:], rstmp[:], link)
                if due(F_USES * (s - 1) + 1):
                    dve.wait_ge(f_filled, F_USES * (s - 1) + 1)
                nc.vector.tensor_scalar(xn[:], xt[:], mv[:, 0:1], rs[:], ALU.subtract, ALU.mult).then_inc(xn_ready, 1)

            def solve(s, n, g, update):
                adds = ADDS_BEFORE
                base, made = SOLVE_OPS * s, [0]

                def link(ins, back=0):
                    made[0] += 1
                    ins.then_inc(solve_chain, 1)
                    dve.wait_ge(solve_chain, base + made[0] - back)

                dve.wait_ge(*dma_of(qp_in, n, g, 0))
                dve.wait_ge(*dma_of(kp_in, n, g, 0))
                dve.wait_ge(*dma_of(vb_in, n, g, 0))
                dve.wait_ge(*dma_of(ab_in, n, g, 0))
                dve.wait_ge(*dma_of(nb_in, n, g, 0))
                for dots in (qp[:, g, :, DV:ROW], kp[:, :, DV:ROW]):
                    link(nc.vector.tensor_tensor(dots, dots, nb[:, g:g + 1, :].to_broadcast([128, C, C]), ALU.mult))
                for r in range(C):
                    w = C - 1 - r
                    rows = kp[:, r + 1:C, 0:DV]
                    link(nc.vector.tensor_tensor(vb[:, g, r, :], kp[:, r, 0:DV], vb[:, g, r, :], ALU.subtract), 1)
                    if w:
                        link(nc.vector.tensor_tensor(rows, rows, ab[:, g, r:r + 1, :].to_broadcast([128, w, DV]), ALU.mult), 1)
                        link(nc.vector.tensor_tensor(
                            t2[:, 0:w], kp[:, r + 1:C, DV + r:DV + r + 1].to_broadcast([128, w, DV]),
                            vb[:, g, r:r + 1, :].to_broadcast([128, w, DV]), ALU.mult))
                        link(nc.vector.tensor_tensor(rows, rows, t2[:, 0:w], ALU.add))
                    for u in range(adds, min(adds + ADDS_PER_ROW, 8)):
                        if update:
                            state(s - 1, 1 - g, u)
                        adds += 1
                dve.wait_ge(pool_chain, POOL_OPS * s + DECAY_OPS + 2)
                dve.wait_ge(solve_chain, base + made[0])
                link(nc.vector.tensor_tensor(eb[:], vb[:, g], eb[:], ALU.mult))
                assert made[0] == SOLVE_OPS

            def slot(s, n, g, lo, hi):
                update, front = updates(lo - 1, hi - 1), valid(lo + 1, hi + 1)
                if front:
                    conv(s + 1, 0)
                    conv(s + 1, 1)
                taps = iter(range(2, TAP_GROUPS))

                def more_taps():
                    k = next(taps, None)
                    if k is not None and front:
                        conv(s + 1, k)

                if valid(lo + 2, hi + 2):
                    norm(s + 2, n + 1, g, more_taps)
                for _ in range(TAP_GROUPS):
                    more_taps()
                if front:
                    for j in range(3):
                        silu(s + 1, 1 - g, j)
                if update:
                    decay(s - 1, n - 1 + g, 1 - g)
                    for u in range(ADDS_BEFORE):
                        state(s - 1, 1 - g, u)
                if valid(lo, hi):
                    solve(s, n, g, update)

            slot_loop(dve, slot, FIRST, LAST, LOOP)


WORK_BANKS = 3
HALVES = 2 * NT
SCORES_IN = (4, 3, 3, 2, 2, 2, 0, 0)
NORMS_IN_HALF = 2
XN_HALF, GATES_HALF, EXPERTS_HALF, WEIGHTS_HALF, GATED_HALF = 0, 1, 3, 5, 6


PROJECTIONS = [(use, t) for use in ("v", "rest") for t in range(NT // 2)]


def scores_in(half):
    first = sum(SCORES_IN[:half])
    return range(first, first + SCORES_IN[half])


def turn_uses(attention, tiles):
    uses = []
    if attention:
        uses += PROJECTIONS + [("score", 0, n) for n in range(4 * NT)] + [("max", 0, i) for i in range(4)]
    for j in range(NT):
        for half in range(HALVES):
            if attention and j + 1 < NT:
                uses += [("score", j + 1, n) for n in scores_in(half)]
            if tiles and half == XN_HALF:
                uses += [("xn", j)]
            if tiles and half == GATES_HALF:
                uses += [("gate", j, 0), ("gate", j, 1), ("small", j)]
            if tiles and half == GATED_HALF:
                uses += [("lora", j), ("og", j, 0), ("og", j, 1)]
        if tiles:
            uses += [("x1", j)]
        if attention and j + 1 < NT:
            uses += [("max", j + 1, i) for i in range(4)]
        if attention:
            uses += [("heads", j)]
    if tiles:
        uses += [("xn2", k) for k in range(2)] + [("qk", m) for m in range(QK_TILES)]
    if attention:
        uses += [("joined", t) for t in range(NT // 2)] + [("out", t) for t in range(NT)]
    return uses


class Turn:

    def __init__(self, b, attention, tiles):
        names = turn_uses(attention, tiles)
        self.place, count = {}, [0] * WORK_BANKS
        for n, name in enumerate(names):
            bank = n % WORK_BANKS
            self.place[name] = bank, count[bank]
            count[bank] += 1
        first, full = ([len(turn_uses(*w)[k::WORK_BANKS]) for k in range(WORK_BANKS)] for w in ((False, True), (True, True)))
        self.before = [0] * WORK_BANKS if not attention else [first[k] + full[k] * b for k in range(WORK_BANKS)]

    def count(self, name):
        bank, n = self.place[name]
        return bank, self.before[bank] + n


def turns(engine, body):
    body(-1, Turn(-1, False, True), False, True, True)
    body(0, Turn(0, True, True), True, True, True)
    with engine.Fori(1, B - 2) as b:
        body(b, Turn(b, True, True), True, True, True)
    body(B - 2, Turn(B - 2, True, True), True, True, False)
    body(B - 1, Turn(B - 1, True, False), True, False, False)


def layer0_end_and_layer1(nc, ins, o_dram, out):
    x = ins["L0_attn_x"]
    part_dram = [nc.dram_tensor(f"part_dram{m}", [PARTS, D1, 8, T], bf16).ap() for m in range(QK_TILES)]
    with ExitStack() as ctx:
        def sb(name, shape, dt=f32):
            return ctx.enter_context(nc.sbuf_tensor(name, shape, dt))

        def ps(name, shape):
            return ctx.enter_context(nc.psum_tensor(name, shape, f32))

        def sem(name):
            return ctx.enter_context(nc.semaphore(name))

        ident = sb("ident2", [128, 128])
        ident_b = sb("ident_b", [128, 128], bf16)
        ones = sb("ones2", [1, 128])
        iota = sb("iota", [128, E])
        wg = sb("wg", [128, 2, HD])
        wsm = sb("wsm", [128, 2, E + ER])
        wbase = sb("wbase", [128, 2, HID])
        wo = sb("wo", [128, HP, HID])
        lup = sb("lup", [128, HID])
        gate_b = sb("gate_b", [1, E + ER])
        b_base = sb("b_base", [128, HID])
        ln_w = sb("ln_w", [128, DV])
        ln_b = sb("ln_b", [128, DV])
        wqk = sb("wqk", [128, 2, QK_TILES, 128])
        bqk = sb("bqk", [128, QK_TILES])
        wv = sb("wv", [128, 2, HID])
        bv = sb("bv", [128, HID])
        w_out = sb("w_out", [128, 2, HID])
        b_out = sb("b_out", [128, HID])
        bias = sb("bias", [128, HID])
        kern = sb("kern", [128, 2, HID])
        aT = sb("aT", [16, HID])
        bmat = sb("bmat", [16, HID])
        wffn = sb("wffn", [128, 2, HID])
        pmax = sb("pmax", [128, 1])
        gmax = sb("gmax", [1, 1])
        scale = sb("scale", [128, 2])

        px = sb("px", [128, 2, HID])
        pxb = sb("pxb", [128, 2, HID])
        ot = sb("ot", [128, 2, H, DV])
        xn = sb("xn_b", [128, HID])
        xnT = sb("xnT_b", [128, 2, 128])
        gl = sb("gl", [128, H, DV])
        lh = sb("lh", [128, E + ER])
        hw = sb("hw", [128, ER])
        hwT = sb("hwT", [128, 128])
        top = sb("top", [128, 8])
        topi = sb("topi", [128, 8], u32)
        topf = sb("topf", [128, 2])
        dtop = sb("dtop", [128, 1])
        topt = sb("topt", [128, 2])
        topw = sb("topw", [128, 2])
        wexp = sb("wexp", [128, 2, E])
        ogT = sb("ogT", [128, HP, 128])
        bst = sb("bst_b", [128, H + 1, 6])
        mv = sb("mv_b", [128, 2])
        m2 = sb("m2", [128, H])
        dm = sb("dm", [128, H])
        vs = sb("vs", [128, H])
        var = sb("var_b", [128, H + 1])
        rs = sb("rs_b", [128, H + 1])
        rstmp = sb("rstmp_b", [128, H + 1])
        nmr = sb("nmr", [128, H])
        x1 = sb("x1", [128, NT, HID])

        x1b = sb("x1b", [128, NT, HID])
        bst2 = sb("bst2", [128, NT, 6])
        mv2 = sb("mv2", [128, NT, 2])
        var2 = sb("var2", [128, NT])
        rs2 = sb("rs2", [128, NT])
        rstmp2 = sb("rstmp2", [128, NT])
        xn2 = sb("xn2", [128, NT, HID])
        xn2T = sb("xn2T", [128, 2, T])
        parts = sb("parts", [128, QK_TILES, PARTS, T], bf16)
        left = sb("left", [128, QK_TILES, T])
        qs = sb("qs", [128, H1, T], bf16)
        ks = sb("ks", [128, H1, T], bf16)
        v = sb("v", [128, NT, H1, 32])
        rest = sb("rest", [128, NT, HID])
        nmax = sb("nmax", [128, 4 * NT])
        nleft = sb("nleft", [128, 4 * NT])
        npart = sb("npart", [128, 4 * NT, PARTS], bf16)
        pt = sb("pt", [128, 2, 4, T])
        oa = sb("oa", [128, T])
        rden = sb("rden", [128, NT * 4])
        ao = sb("ao", [128, NT, H1, D1])
        aoT = sb("aoT", [128, 2, T])
        ob = sb("ob", [128, 2, HID])

        w_bank = [ps(f"w_bank{i}", [128, 512]) for i in range(WORK_BANKS)]
        e_bank = [ps(f"e_bank{i}", [128, 2, 512]) for i in range(2)]
        o_bank = ps("o_bank", [128, 512])

        consts_in, ident_done, init_done, init_chain, init_pe = map(
            sem, ("consts_in2", "ident_done2", "init_done2", "init_chain", "init_pe"))
        w_filled = [sem(f"w_filled{i}") for i in range(WORK_BANKS)]
        w_freed = [sem(f"w_freed{i}") for i in range(WORK_BANKS)]
        px_in, ot_in = [sem(f"px_in{i}") for i in range(2)], [sem(f"ot_in{i}") for i in range(2)]
        stat_chain, tile_ready, gate_chain, gates_tanh, normed, affine = map(
            sem, ("stat_chain", "tile_ready", "gate_chain", "gates_tanh", "normed", "affine"))
        affine_chain, og_done, pxb_done, x1b_done = map(sem, ("affine_chain", "og_done", "pxb_done", "x1b_done"))
        hw_ready, xn2_chain, xn2_ready, nmax_chain, nmax_ready = map(
            sem, ("hw_ready", "xn2_chain", "xn2_ready", "nmax_chain", "nmax_ready"))
        e_filled, e_freed, pv_done, oa_done, joined, rden_done = map(
            sem, ("e_filled", "e_freed", "pv_done", "oa_done", "joined", "rden_done"))
        part_chain, parts_ready, second_part = map(sem, ("part_chain", "parts_ready", "second_part"))
        first_part = sem("first_part")
        part_wr = [sem(f"part_wr{m}") for m in range(QK_TILES)]
        stack_in = [sem(f"stack_in{m}") for m in range(QK_TILES)]
        out_wr = [sem(f"out_wr{i}") for i in range(2)]
        out_done = sem("out_done")
        sp_passed, pe_passed, dve_passed = map(sem, ("sp_passed2", "pe_passed2", "dve_passed2"))
        CONSTS = 19
        STAT_OPS = 3 + 7 + 14
        GATE_OPS = 8
        XN2_OPS = 2 * NT + 1 + 14

        block = ctx.enter_context(nc.Block())

        def x1_stats(bt, j):
            if j < 0:
                return XN2_OPS * (bt - 1) + 2 * (NT + j) + 1
            return XN2_OPS * bt + 2 * j + 1

        @block.sync
        def _(sp):
            def row(a):
                return a.rearrange("(a n) -> a n", a=1)

            def tiles(a):
                return a.rearrange("(k p) n -> p k n", p=128)

            def spread(a):
                return row(a).to_broadcast([128, HID])

            loads = (
                (wg[:], tiles(ins["wg"])), (wsm[:], tiles(ins["wsm"])), (wbase[:], tiles(ins["wbase"])),
                (wo[:], tiles(ins["wo"])), (lup[:], ins["lup"]), (gate_b[:, 0:E], row(ins["L0_ffn_gate_b"])),
                (b_base[:], spread(ins["L0_ffn_b_base"])),
                (ln_w[:], row(ins["L0_attn_ln_w"]).to_broadcast([128, DV])),
                (ln_b[:], row(ins["L0_attn_ln_b"]).to_broadcast([128, DV])),
                (wqk[:], ins["wqk"].rearrange("(k p) (m n) -> p k m n", p=128, n=128)), (bqk[:], ins["bqk"]),
                (wv[:], tiles(ins["wv"])), (bv[:], spread(ins["bv"])),
                (w_out[:], tiles(ins["L1_attn_w_out"])), (b_out[:], spread(ins["L1_attn_b_out"])),
                (bias[:], spread(ins["L1_ffn_bias"])), (kern[:], tiles(ins["L1_ffn_kernel"])),
                (aT[:], ins["aT"]), (bmat[:], ins["L1_ffn_b"]),
            )
            assert len(loads) == CONSTS
            for tile, src in loads:
                sp.dma_start(tile, src).then_inc(consts_in, 16)

            def write_parts(m, done):
                sp.wait_ge(parts_ready, done + m + 1)
                held(sp, sp_passed)
                for c in range(PARTS):
                    sp.dma_start(part_dram[m][c].rearrange("d h t -> h d t"), parts[:, m, c, :]).then_inc(part_wr[m], 16)

            def read_stack(m, b):
                sp.wait_ge(part_wr[m], 16 * PARTS * (b + 2))
                held(sp, sp_passed)
                h = 8 * (m // 2)
                row_ = 0
                for runs in (PARTS, PARTS - 1, 1):
                    rows = slice(row_, row_ + D1 * runs)
                    if m % 2 == 0:
                        src = part_dram[m][PARTS - runs:PARTS - runs + 1].to_broadcast([runs, D1, 8, T])
                        sp.dma_start(qs[rows, h:h + 8, :], src).then_inc(stack_in[m], 16)
                    else:
                        sp.dma_start(ks[rows, h:h + 8, :], part_dram[m][0:runs]).then_inc(stack_in[m], 16)
                    row_ += D1 * runs

            def body(b, turn, attention, tiles_, more):
                def load(bt, j):
                    if due(NT * bt + j - 1):
                        sp.wait_ge(xn2_chain, x1_stats(bt, j - 2))
                    held(sp, sp_passed)
                    sp.dma_start(px[:, j % 2], x[bass.ds(bt, 1), 128 * j:128 * j + 128]).then_inc(px_in[j % 2], 16)
                    sp.dma_start(ot[:, j % 2], o_dram[128 * j:128 * j + 128, bass.ds(bt, 1)]).then_inc(ot_in[j % 2], 16)

                if tiles_:
                    if not attention:
                        load(0, 0)
                    for j in range(1, NT):
                        load(b + 1, j)
                    if more:
                        load(b + 2, 0)
                    for first in range(0, QK_TILES, 2):
                        for m in (first, first + 1):
                            write_parts(m, QK_TILES * (b + 1))
                        for m in (first, first + 1):
                            read_stack(m, b)
            turns(sp, body)

        @block.gpsimd
        def _(pool):
            nc.gpsimd.memset(ident[:], 0.0).then_inc(ident_done, 1)
            pool.wait_ge(ident_done, 1)
            nc.gpsimd.affine_select(out=ident[:], in_=ident[:], compare_op=ALU.not_equal, fill=1.0, base=0,
                                    pattern=[[-1, 128]], channel_multiplier=1).then_inc(ident_done, 1)
            pool.wait_ge(init_done, 1)

            def body(b, turn, attention, tiles_, more):
                if not tiles_:
                    return
                bt = b + 1
                for j in range(NT):
                    t = NT * bt + j
                    o = ot[:, j % 2]
                    pool.wait_ge(px_in[j % 2], 16 * (2 * bt + j // 2 + 1))
                    if due(t - 1):
                        pool.wait_ge(xn2_chain, x1_stats(bt, j - 2))
                    nc.gpsimd.tensor_tensor(pxb[:, j % 2], px[:, j % 2], b_base[:], ALU.add).then_inc(pxb_done, 1)
                    pool.wait_ge(normed, t + 1)
                    nc.gpsimd.tensor_tensor(o, o, ln_w[:].unsqueeze(1).to_broadcast([128, H, DV]), ALU.mult).then_inc(affine_chain, 1)
                    pool.wait_ge(affine_chain, t + 1)
                    nc.gpsimd.tensor_tensor(o, o, ln_b[:].unsqueeze(1).to_broadcast([128, H, DV]), ALU.add).then_inc(affine, 1)
                    pool.wait_ge(xn2_chain, x1_stats(bt, j))
                    nc.gpsimd.tensor_tensor(x1b[:, j], x1[:, j], bias[:], ALU.add).then_inc(x1b_done, 1)
            turns(pool, body)

        @block.tensor
        def _(pe):
            pe.wait_ge(consts_in, 16 * CONSTS)
            pe.wait_ge(ident_done, 2)
            pe.wait_ge(init_chain, 1)
            nc.tensor.transpose(w_bank[0][0:1, 0:128], pmax[:], ident[:]).then_inc(init_pe, 1)
            pe.wait_ge(init_chain, 3)
            nc.tensor.matmul(w_bank[1][:, 0:1], ones[:], gmax[:], start=True, stop=True).then_inc(init_pe, 1)
            for k in range(2):
                mm = nc.tensor.matmul(w_bank[2][:, HID * k:HID * k + HID], aT[:, 128 * k:128 * k + 128], bmat[:], start=True, stop=True)
            mm.then_inc(init_pe, 1)
            pe.wait_ge(init_done, 1)

            def body(b, turn, attention, tiles_, more):
                bt = b + 1

                def freed_before(*name):
                    bank, n = turn.count(name)
                    return w_freed[bank], n

                def emptied(*name):
                    bank, n = turn.count(name)
                    return w_freed[bank], n + 1

                def place(*name):
                    bank = turn.count(name)[0]
                    return w_bank[bank], w_filled[bank]

                def scores(j, which):
                    for n in which:
                        t, h = n // 4, 4 * j + n % 4
                        bank, filled = place("score", j, n)
                        if due(freed_before("score", j, n)[1]):
                            pe.wait_ge(*freed_before("score", j, n))
                        nc.tensor.matmul(bank[:], qs[0:ROWS, h, 128 * t:128 * t + 128], ks[0:ROWS, h, :],
                                         start=True, stop=True).then_inc(filled, 1)

                def maxima(j):
                    pe.wait_ge(nmax_ready, NT * b + j + 1)
                    for i in range(4):
                        bank, filled = place("max", j, i)
                        pe.wait_ge(*freed_before("max", j, i))
                        for t in range(NT):
                            mm = nc.tensor.matmul(bank[ROWS:ROWS + PARTS, 128 * t:128 * t + 128], npart[:, 4 * t + i, :], ident_b[:],
                                                  start=True, stop=True, tile_position=(0, ROWS))
                        mm.then_inc(filled, 1)

                def context(j, kt):
                    pe.wait_ge(e_freed, HALVES * (NT * b + j) + 2 * kt + 2)
                    if kt == 0 and due(NT * b + j):
                        pe.wait_ge(oa_done, NT * b + j)
                    for i in range(4):
                        mm = nc.tensor.matmul(o_bank[32 * i:32 * i + 32, :], v[:, kt, 4 * j + i, :], pt[:, kt % 2, i, :],
                                              start=kt == 0, stop=kt == NT - 1, tile_position=(0, 32 * i))
                    mm.then_inc(pv_done, 1)

                def exponents(j, half):
                    kt, pr = half // 2, half % 2
                    if kt:
                        pe.wait_ge(e_freed, HALVES * (NT * b + j) + half - 1)
                    for i in (2 * pr, 2 * pr + 1):
                        h = 4 * j + i
                        mm = nc.tensor.matmul(e_bank[pr][:, i % 2, :], ks[0:ROWS + PARTS, h, 128 * kt:128 * kt + 128],
                                              qs[0:ROWS + PARTS, h, :], start=True, stop=True)
                    mm.then_inc(e_filled, 1)

                def heads(j):
                    bank, filled = place("heads", j)
                    pe.wait_ge(*freed_before("heads", j))
                    pe.wait_ge(oa_done, NT * b + j + 1)
                    for t in range(NT):
                        mm = nc.tensor.transpose(bank[:, 128 * t:128 * t + 128], oa[:, 128 * t:128 * t + 128], ident[:])
                    mm.then_inc(filled, 1)

                def tile_rows(j):
                    bank, filled = place("xn", j)
                    if due(freed_before("xn", j)[1]):
                        pe.wait_ge(*freed_before("xn", j))
                    pe.wait_ge(tile_ready, NT * bt + j + 1)
                    for k in range(2):
                        mm = nc.tensor.transpose(bank[:, 128 * k:128 * k + 128], xn[:, 128 * k:128 * k + 128], ident[:])
                    mm.then_inc(filled, 1)

                def gates(j):
                    pe.wait_ge(*emptied("xn", j))
                    for h in range(2):
                        bank, filled = place("gate", j, h)
                        if due(freed_before("gate", j, h)[1]):
                            pe.wait_ge(*freed_before("gate", j, h))
                        for k in range(2):
                            mm = nc.tensor.matmul(bank[:], xnT[:, k, :], wg[:, k, 512 * h:512 * h + 512], start=k == 0, stop=k == 1)
                        mm.then_inc(filled, 1)
                    bank, filled = place("small", j)
                    pe.wait_ge(*freed_before("small", j))
                    for k in range(2):
                        nc.tensor.matmul(bank[:, 0:E + ER], xnT[:, k, :], wsm[:, k, :], start=k == 0, stop=False)
                    nc.tensor.matmul(bank[:, 0:E + ER], ones[:], gate_b[:], start=False, stop=True).then_inc(filled, 1)

                def gated(j):
                    bank, filled = place("lora", j)
                    pe.wait_ge(*freed_before("lora", j))
                    pe.wait_ge(hw_ready, NT * bt + j + 1)
                    held(pe, pe_passed)
                    nc.tensor.transpose(bank[0:ER, 0:128], hw[:], ident[:]).then_inc(filled, 1)
                    pe.wait_ge(og_done, NT * bt + j + 1)
                    for h in range(2):
                        bank, filled = place("og", j, h)
                        pe.wait_ge(*freed_before("og", j, h))
                        for i in range(4):
                            m = 4 * h + i
                            mm = nc.tensor.transpose(bank[:, 128 * i:128 * i + 128], ot[:, j % 2, 2 * m:2 * m + 2, :].rearrange("p h i -> p (h i)"), ident[:])
                        mm.then_inc(filled, 1)

                def new_rows(j):
                    bank, filled = place("x1", j)
                    pe.wait_ge(*freed_before("x1", j))
                    for k in range(2):
                        nc.tensor.matmul(bank[:, 0:HID], xnT[:, k, :], wbase[:, k, :], start=k == 0, stop=False)
                    pe.wait_ge(*emptied("lora", j))
                    nc.tensor.matmul(bank[:, 0:HID], hwT[:], lup[:], start=False, stop=False)
                    for h in range(2):
                        pe.wait_ge(*emptied("og", j, h))
                        for m in range(4 * h, 4 * h + 4):
                            mm = nc.tensor.matmul(bank[:, 0:HID], ogT[:, m, :], wo[:, m, :], start=False, stop=m == HP - 1)
                    mm.then_inc(filled, 1)

                def project(use, t):
                    bank, filled = place(use, t)
                    pe.wait_ge(*freed_before(use, t))
                    w = wv if use == "v" else wffn
                    for i in range(2):
                        for k in range(2):
                            mm = nc.tensor.matmul(bank[:, HID * i:HID * i + HID], xn2T[:, k, 128 * (2 * t + i):128 * (2 * t + i) + 128],
                                                  w[:, k, :], start=k == 0, stop=k == 1)
                    mm.then_inc(filled, 1)

                if attention:
                    for use in PROJECTIONS:
                        project(*use)
                    for m in (0, 1):
                        pe.wait_ge(stack_in[m], 16 * PARTS * (b + 1))
                    scores(0, range(4 * NT))
                    maxima(0)
                for j in range(NT):
                    if attention:
                        for i in range(4):
                            pe.wait_ge(*emptied("max", j, i))
                        if j == 1:
                            for m in (2, 3):
                                pe.wait_ge(stack_in[m], 16 * PARTS * (b + 1))
                    for half in range(HALVES):
                        if attention:
                            exponents(j, half)
                            if half % 2 and half > 1:
                                context(j, half // 2 - 1)
                            if j + 1 < NT:
                                scores(j + 1, scores_in(half))
                        if tiles_ and half == XN_HALF:
                            tile_rows(j)
                        if tiles_ and half == GATES_HALF:
                            gates(j)
                        if tiles_ and half == GATED_HALF:
                            gated(j)
                    if tiles_:
                        new_rows(j)
                    if attention:
                        context(j, NT - 1)
                        if j + 1 < NT:
                            maxima(j + 1)
                        heads(j)
                if tiles_:
                    pe.wait_ge(xn2_ready, NT * (b + 2))
                    for k in range(2):
                        bank, filled = place("xn2", k)
                        pe.wait_ge(*freed_before("xn2", k))
                        for t in range(NT):
                            mm = nc.tensor.transpose(bank[:, 128 * t:128 * t + 128], xn2[:, t, 128 * k:128 * k + 128], ident[:])
                        mm.then_inc(filled, 1)
                    for k in range(2):
                        pe.wait_ge(*emptied("xn2", k))
                    for m in range(QK_TILES):
                        bank, filled = place("qk", m)
                        pe.wait_ge(*freed_before("qk", m))
                        for k in range(2):
                            mm = nc.tensor.matmul(bank[:], wqk[:, k, m, :], xn2T[:, k, :], start=k == 0, stop=k == 1)
                        mm.then_inc(filled, 1)
                if attention:
                    pe.wait_ge(joined, NT * (b + 1))
                    for t in range(NT // 2):
                        bank, filled = place("joined", t)
                        pe.wait_ge(*freed_before("joined", t))
                        for i in range(2):
                            for k in range(2):
                                mm = nc.tensor.transpose(bank[:, 256 * i + 128 * k:256 * i + 128 * k + 128],
                                                         ao[:, 2 * t + i].rearrange("p h d -> p (h d)")[:, 128 * k:128 * k + 128], ident[:])
                        mm.then_inc(filled, 1)
                    for t in range(NT):
                        bank, filled = place("out", t)
                        pe.wait_ge(*freed_before("out", t))
                        pe.wait_ge(*emptied("joined", t // 2))
                        for k in range(2):
                            mm = nc.tensor.matmul(bank[:, 0:HID], aoT[:, k, 128 * t:128 * t + 128], w_out[:, k, :], start=k == 0, stop=k == 1)
                        mm.then_inc(filled, 1)
            turns(pe, body)

        @block.scalar
        def _(act):
            act.wait_ge(init_done, 1)

            def body(b, turn, attention, tiles_, more):
                bt = b + 1

                def filled(*name):
                    bank, n = turn.count(name)
                    return w_filled[bank], n + 1

                def place(*name):
                    bank = turn.count(name)[0]
                    return w_bank[bank], w_freed[bank]

                def maxima(j):
                    for i in (2, 3):
                        bank, freed = place("max", j, i)
                        act.wait_ge(*filled("max", j, i))
                        nc.scalar.activation(qs[ROWS:ROWS + PARTS, 4 * j + i, :], bank[ROWS:ROWS + PARTS, :], ACT.Copy).then_inc(freed, 1)

                def exponentials(j, half):
                    kt, pr = half // 2, half % 2
                    act.wait_ge(e_filled, HALVES * (NT * b + j) + half + 1)
                    if kt >= 2:
                        act.wait_ge(pv_done, NT * (NT * b + j) + kt - 1)
                    nc.scalar.activation(pt[:, kt % 2, 2 * pr:2 * pr + 2], e_bank[pr][:], ACT.Exp, scale=float(D1) ** -0.5).then_inc(e_freed, 1)

                def tile_rows(j):
                    bank, freed = place("xn", j)
                    act.wait_ge(*filled("xn", j))
                    nc.scalar.activation(xnT[:].rearrange("p k t -> p (k t)"), bank[:, 0:256], ACT.Copy).then_inc(freed, 1)

                def gates(j):
                    if due(NT * bt + j):
                        act.wait_ge(og_done, NT * bt + j)
                    for h in range(2):
                        bank, freed = place("gate", j, h)
                        act.wait_ge(*filled("gate", j, h))
                        nc.scalar.activation(gl[:, 8 * h:8 * h + 8].rearrange("p h i -> p (h i)"), bank[:], ACT.Tanh, scale=0.5).then_inc(freed, 1)
                    bank, freed = place("small", j)
                    act.wait_ge(*filled("small", j))
                    if due(NT * bt + j):
                        act.wait_ge(hw_ready, NT * bt + j)
                    nc.scalar.activation(lh[:], bank[:, 0:E + ER], ACT.Copy).then_inc(freed, 1)

                def norm_heads(j, quarter):
                    o = ot[:, j % 2]
                    if quarter == 0:
                        act.wait_ge(tile_ready, NT * bt + j + 1)
                    for h in range(4 * quarter, 4 * quarter + 4):
                        last = nc.scalar.activation(o[:, h, :], o[:, h, :], ACT.Identity, bias=nmr[:, h:h + 1], scale=rs[:, h + 1:h + 2])
                    if quarter == 3:
                        last.then_inc(normed, 1)

                def top_weights(j):
                    act.wait_ge(gate_chain, GATE_OPS * (NT * bt + j) + 4)
                    nc.scalar.activation(topt[:, 0:1], dtop[:], ACT.Tanh, scale=-0.5)
                    nc.scalar.activation(topt[:, 1:2], dtop[:], ACT.Tanh, scale=0.5).then_inc(gates_tanh, 1)

                def gated(j):
                    bank, freed = place("lora", j)
                    act.wait_ge(*filled("lora", j))
                    nc.scalar.activation(hwT[0:ER, :], bank[0:ER, 0:128], ACT.Copy).then_inc(freed, 1)
                    for h in range(2):
                        bank, freed = place("og", j, h)
                        act.wait_ge(*filled("og", j, h))
                        nc.scalar.activation(ogT[:, 4 * h:4 * h + 4].rearrange("p m t -> p (m t)"), bank[:], ACT.Copy).then_inc(freed, 1)

                if attention:
                    maxima(0)
                for j in range(NT):
                    for half in range(HALVES):
                        if attention:
                            exponentials(j, half)
                        if tiles_ and half < 4 // NORMS_IN_HALF:
                            for quarter in range(NORMS_IN_HALF * half, NORMS_IN_HALF * half + NORMS_IN_HALF):
                                norm_heads(j, quarter)
                        if tiles_ and half == XN_HALF:
                            tile_rows(j)
                        if tiles_ and half == GATES_HALF:
                            gates(j)
                        if tiles_ and half == EXPERTS_HALF:
                            top_weights(j)
                        if tiles_ and half == GATED_HALF:
                            gated(j)
                    if attention:
                        act.wait_ge(pv_done, NT * (NT * b + j + 1))
                        nc.scalar.activation(oa[:], o_bank[:], ACT.Copy).then_inc(oa_done, 1)
                        if j + 1 < NT:
                            maxima(j + 1)
                if tiles_:
                    for k in range(2):
                        bank, freed = place("xn2", k)
                        act.wait_ge(*filled("xn2", k))
                        nc.scalar.activation(xn2T[:, k, :], bank[:], ACT.Copy).then_inc(freed, 1)

                    def second(m):
                        act.wait_ge(part_chain, QK_TILES * bt + m + 1)
                        nc.scalar.activation(parts[:, m, 1, :], left[:, m], ACT.Copy).then_inc(second_part, 1)

                    for m in range(QK_TILES):
                        bank, freed = place("qk", m)
                        act.wait_ge(*filled("qk", m))
                        if due(16 * PARTS * bt):
                            act.wait_ge(part_wr[m], 16 * PARTS * bt)
                        nc.scalar.activation(parts[:, m, 0, :], bank[:], ACT.Identity, bias=bqk[:, m:m + 1]).then_inc(first_part, 1)
                        if m:
                            second(m - 1)
                    second(QK_TILES - 1)
                if attention:
                    for t in range(NT // 2):
                        bank, freed = place("joined", t)
                        act.wait_ge(*filled("joined", t))
                        nc.scalar.activation(aoT[:, :, 256 * t:256 * t + 256].rearrange("p k (i q) -> p i k q", i=2),
                                             bank[:].rearrange("p (i k q) -> p i k q", i=2, k=2), ACT.Copy).then_inc(freed, 1)
                    for t in range(NT):
                        act.wait_ge(out_done, NT * b + t + 1)
                        act.dma_start(out[bass.ds(b, 1), 128 * t:128 * t + 128], ob[:, t % 2]).then_inc(out_wr[t % 2], 16)
            turns(act, body)
            for i in range(2):
                act.wait_ge(out_wr[i], 16 * 2 * B)

        @block.vector
        def _(dve):
            chain = [0]

            def start(ins_):
                chain[0] += 1
                ins_.then_inc(init_chain, 1)
                dve.wait_ge(init_chain, chain[0])

            dve.wait_ge(consts_in, 16 * CONSTS)
            start(nc.vector.tensor_reduce(pmax[:], kern[:], AX.XY, ALU.max, apply_absolute_value=True))
            dve.wait_ge(init_pe, 1)
            start(nc.vector.memset(ones[:], 1.0))
            start(nc.vector.reduce_max(gmax[:], w_bank[0][0:1, 0:128], AX.X))
            dve.wait_ge(init_pe, 2)
            start(nc.vector.tensor_scalar(scale[:, 0:1], w_bank[1][:, 0:1], 1.0 / 7.0, None, ALU.mult))
            start(nc.vector.reciprocal(scale[:, 1:2], scale[:, 0:1]))
            start(nc.vector.tensor_scalar(wffn[:], kern[:], scale[:, 1:2], None, ALU.mult))
            start(nc.vector.tensor_scalar(wffn[:], wffn[:], ROUND, None, ALU.add))
            start(nc.vector.tensor_scalar(wffn[:], wffn[:], ROUND, -8.0, ALU.subtract, ALU.max))
            start(nc.vector.tensor_scalar(wffn[:], wffn[:], 7.0, scale[:, 0:1], ALU.min, ALU.mult))
            dve.wait_ge(init_pe, 3)
            start(nc.vector.tensor_tensor(wffn[:].rearrange("p k n -> p (k n)"), wffn[:].rearrange("p k n -> p (k n)"), w_bank[2][:], ALU.add))
            start(nc.vector.tensor_tensor(bias[:], bias[:], b_out[:], ALU.add))
            start(nc.vector.tensor_scalar(ln_w[:], ln_w[:], 0.5, None, ALU.mult))
            start(nc.vector.tensor_scalar(ln_b[:], ln_b[:], 0.5, None, ALU.mult))
            start(nc.vector.tensor_scalar(lup[:], lup[:], 1.0 / R, None, ALU.mult))
            start(nc.vector.memset(gate_b[:, E:], 0.0))
            start(nc.vector.memset(hwT[:], 0.0))
            dve.wait_ge(ident_done, 2)
            start(nc.vector.tensor_copy(ident_b[:], ident[:]))
            start(nc.vector.memset(ks[ROWS:ROWS + PARTS], 1.0))
            start(nc.vector.memset(v[:, :, :, D1:], 0.0))
            start(nc.vector.memset(v[:, :, :, D1:D1 + 1], 1.0))
            for e in range(E):
                start(nc.vector.memset(iota[:, e:e + 1], float(e)))
            nc.vector.memset(rstmp[:], 0.0).then_inc(init_done, 1)
            dve.wait_ge(init_done, 1)

            def linker(sem_, base):
                made = [0]

                def link(ins_):
                    made[0] += 1
                    ins_.then_inc(sem_, 1)
                    dve.wait_ge(sem_, base + made[0])
                return link

            def body(b, turn, attention, tiles_, more):
                bt = b + 1

                def filled(*name):
                    bank, n = turn.count(name)
                    return w_filled[bank], n + 1

                def emptied(*name):
                    bank, n = turn.count(name)
                    return w_freed[bank], n + 1

                def place(*name):
                    bank = turn.count(name)[0]
                    return w_bank[bank], w_freed[bank]

                def scores(j, which):
                    for n in which:
                        bank, freed = place("score", j, n)
                        dve.wait_ge(*filled("score", j, n))
                        nc.vector.tensor_reduce(nmax[:, n:n + 1], bank[:], AX.X, ALU.max, negate=True).then_inc(freed, 1)

                def maxima(j):
                    link = linker(nmax_chain, 3 * (NT * b + j))
                    for n in range(4 * NT - WORK_BANKS, 4 * NT):
                        dve.wait_ge(*emptied("score", j, n))
                    link(nc.vector.tensor_copy(npart[:, :, 0], nmax[:]))
                    link(nc.vector.tensor_tensor(nleft[:], nmax[:], npart[:, :, 0], ALU.subtract))
                    link(nc.vector.tensor_copy(npart[:, :, 1], nleft[:]))
                    nc.vector.tensor_tensor(npart[:, :, 2], nleft[:], npart[:, :, 1], ALU.subtract).then_inc(nmax_ready, 1)

                def place_maxima(j):
                    for i in (0, 1):
                        bank, freed = place("max", j, i)
                        dve.wait_ge(*filled("max", j, i))
                        nc.vector.tensor_copy(qs[ROWS:ROWS + PARTS, 4 * j + i, :], bank[ROWS:ROWS + PARTS, :]).then_inc(freed, 1)

                def join(j):
                    bank, freed = place("heads", j)
                    dve.wait_ge(*filled("heads", j))
                    o = bank[:].rearrange("p (m c) -> p m c", c=32)
                    nc.vector.reciprocal(rden[:], o[:, :, D1]).then_inc(rden_done, 1)
                    dve.wait_ge(rden_done, NT * b + j + 1)
                    nc.vector.tensor_tensor(ao[:, :, 4 * j:4 * j + 4, :], o[:, :, 0:D1].rearrange("p (t i) d -> p t i d", t=NT),
                                            rden[:].rearrange("p (t i) -> p t i", t=NT).unsqueeze(3).to_broadcast([128, NT, 4, D1]),
                                            ALU.mult).then_inc(freed, 1)
                    dve.wait_ge(*emptied("heads", j))
                    dve.sem_inc(joined, 1)

                def stats(bt, j):
                    t = NT * bt + j
                    link = linker(stat_chain, STAT_OPS * t)
                    dve.wait_ge(px_in[j % 2], 16 * (2 * bt + j // 2 + 1))
                    if due(t):
                        dve.wait_ge(normed, t)
                    link(nc.vector.bn_stats(bst[:, H, :], px[:, j % 2]))
                    held(dve, dve_passed)
                    link(nc.vector.bn_aggr(mv[:], bst[:, H, :]))
                    link(nc.vector.tensor_scalar(var[:, 0:1], mv[:, 1:2], EPS, None, ALU.add))
                    dve.wait_ge(ot_in[j % 2], 16 * (2 * bt + j // 2 + 1))
                    for h in range(H):
                        last = nc.vector.bn_stats(bst[:, h, :], ot[:, j % 2, h, :])
                    link(last)
                    link(nc.vector.tensor_tensor(m2[:], bst[:, 0:H, 1], bst[:, 0:H, 4], ALU.add))
                    link(nc.vector.tensor_tensor(dm[:], bst[:, 0:H, 1], bst[:, 0:H, 4], ALU.subtract))
                    link(nc.vector.tensor_tensor(dm[:], dm[:], dm[:], ALU.mult))
                    link(nc.vector.tensor_tensor(vs[:], bst[:, 0:H, 2], bst[:, 0:H, 5], ALU.add))
                    link(nc.vector.scalar_tensor_tensor(out=vs[:], in0=dm[:], scalar=DV / 4.0, in1=vs[:], op0=ALU.mult, op1=ALU.add))
                    link(nc.vector.tensor_scalar(var[:, 1:], vs[:], 1.0 / DV, EPS, ALU.mult, ALU.add))
                    rsqrt_ops(nc, rs[:], var[:], rstmp[:], link)
                    nc.vector.scalar_tensor_tensor(out=nmr[:], in0=m2[:], scalar=-0.5, in1=rs[:, 1:], op0=ALU.mult, op1=ALU.mult)
                    nc.vector.tensor_scalar(xn[:], px[:, j % 2], mv[:, 0:1], rs[:, 0:1], ALU.subtract, ALU.mult).then_inc(tile_ready, 1)

                def experts(j):
                    t = NT * bt + j
                    link = linker(gate_chain, GATE_OPS * t)
                    dve.wait_ge(*emptied("small", j))
                    held(dve, dve_passed)
                    link(nc.vector.max(top[:], lh[:, 0:E]))
                    held(dve, dve_passed)
                    link(nc.vector.max_index(topi[:], top[:], lh[:, 0:E]))
                    link(nc.vector.tensor_copy(topf[:], topi[:, 0:2]))
                    link(nc.vector.tensor_tensor(dtop[:], top[:, 1:2], top[:, 0:1], ALU.subtract))

                def expert_weights(j):
                    t = NT * bt + j
                    link = linker(gate_chain, GATE_OPS * t + 4)
                    dve.wait_ge(gates_tanh, t + 1)
                    link(nc.vector.tensor_scalar(topw[:], topt[:], 0.5, 0.5, ALU.mult, ALU.add))
                    link(nc.vector.tensor_scalar(wexp[:, 0], iota[:], topf[:, 0:1], topw[:, 0:1], ALU.is_equal, ALU.mult))
                    link(nc.vector.tensor_scalar(wexp[:, 1], iota[:], topf[:, 1:2], topw[:, 1:2], ALU.is_equal, ALU.mult))
                    link(nc.vector.tensor_tensor(wexp[:, 0], wexp[:, 0], wexp[:, 1], ALU.add))
                    nc.vector.tensor_tensor(hw[:].rearrange("p (e r) -> p e r", r=R), lh[:, E:].rearrange("p (e r) -> p e r", r=R),
                                            wexp[:, 0].unsqueeze(2).to_broadcast([128, E, R]), ALU.mult).then_inc(hw_ready, 1)

                def gate(j):
                    dve.wait_ge(affine, NT * bt + j + 1)
                    for h in range(2):
                        dve.wait_ge(*emptied("gate", j, h))
                    o = ot[:, j % 2]
                    nc.vector.scalar_tensor_tensor(out=o, in0=gl[:], scalar=1.0, in1=o, op0=ALU.add, op1=ALU.mult).then_inc(og_done, 1)

                def new_rows(j):
                    bank, freed = place("x1", j)
                    dve.wait_ge(*filled("x1", j))
                    dve.wait_ge(pxb_done, NT * bt + j + 1)
                    if due(NT * b + j + 1):
                        dve.wait_ge(x1b_done, NT * b + j + 1)
                    nc.vector.tensor_tensor(x1[:, j], bank[:, 0:HID], pxb[:, j % 2], ALU.add).then_inc(freed, 1)
                    link = linker(xn2_chain, XN2_OPS * bt + 2 * j)
                    dve.wait_ge(*emptied("x1", j))
                    link(nc.vector.bn_stats(bst2[:, j, :], x1[:, j, :]))
                    held(dve, dve_passed)
                    link(nc.vector.bn_aggr(mv2[:, j, :], bst2[:, j, :]))

                def project(use, t):
                    bank, freed = place(use, t)
                    dve.wait_ge(*filled(use, t))
                    if use == "v":
                        nc.vector.tensor_tensor(v[:, 2 * t:2 * t + 2, :, 0:D1], bank[:].rearrange("p (t h d) -> p t h d", t=2, d=D1),
                                                bv[:].rearrange("p (h d) -> p h d", d=D1).unsqueeze(1).to_broadcast([128, 2, H1, D1]),
                                                ALU.add).then_inc(freed, 1)
                    else:
                        if t == 0:
                            dve.wait_ge(x1b_done, NT * (b + 1))
                        nc.vector.tensor_tensor(rest[:, 2 * t:2 * t + 2].rearrange("p t n -> p (t n)"), bank[:],
                                                x1b[:, 2 * t:2 * t + 2].rearrange("p t n -> p (t n)"), ALU.add).then_inc(freed, 1)

                if attention:
                    for use in PROJECTIONS:
                        project(*use)
                    scores(0, range(4 * NT))
                    maxima(0)
                    place_maxima(0)
                elif tiles_:
                    stats(0, 0)
                for j in range(NT):
                    if attention and j:
                        join(j - 1)
                    for half in range(HALVES):
                        if attention and j + 1 < NT:
                            scores(j + 1, scores_in(half))
                        if tiles_ and half == EXPERTS_HALF:
                            experts(j)
                        if tiles_ and half == WEIGHTS_HALF:
                            expert_weights(j)
                        if tiles_ and half == GATED_HALF:
                            gate(j)
                    if attention and j + 1 < NT:
                        maxima(j + 1)
                    if tiles_ and j + 1 < NT:
                        stats(bt, j + 1)
                    if tiles_:
                        new_rows(j)
                    if attention and j + 1 < NT:
                        place_maxima(j + 1)
                if tiles_:
                    link = linker(xn2_chain, XN2_OPS * bt + 2 * NT)
                    link(nc.vector.tensor_scalar(var2[:], mv2[:, :, 1], EPS, None, ALU.add))
                    rsqrt_ops(nc, rs2[:], var2[:], rstmp2[:], link)
                    for t in range(NT):
                        nc.vector.tensor_scalar(xn2[:, t, :], x1[:, t, :], mv2[:, t, 0:1], rs2[:, t:t + 1], ALU.subtract, ALU.mult).then_inc(xn2_ready, 1)
                if attention:
                    join(NT - 1)
                if more:
                    stats(bt + 1, 0)
                if tiles_:
                    for m in range(QK_TILES):
                        bank, freed = place("qk", m)
                        t = QK_TILES * bt + m
                        dve.wait_ge(first_part, t + 1)
                        if due(t - 1):
                            dve.wait_ge(second_part, t - 1)
                        nc.vector.scalar_tensor_tensor(out=left[:, m], in0=bank[:], scalar=bqk[:, m:m + 1], in1=parts[:, m, 0, :],
                                                       op0=ALU.add, op1=ALU.subtract).then_inc(freed, 1)
                        dve.wait_ge(*emptied("qk", m))
                        dve.sem_inc(part_chain, 1)
                        dve.wait_ge(second_part, t + 1)
                        nc.vector.tensor_tensor(parts[:, m, 2, :], left[:, m], parts[:, m, 1, :], ALU.subtract).then_inc(parts_ready, 1)
                if attention:
                    for t in range(NT):
                        bank, freed = place("out", t)
                        dve.wait_ge(*filled("out", t))
                        if due(16 * (2 * b + t // 2)):
                            dve.wait_ge(out_wr[t % 2], 16 * (2 * b + t // 2))
                        nc.vector.tensor_tensor(ob[:, t % 2], bank[:, 0:HID], rest[:, t], ALU.add).then_inc(freed, 1)
                        dve.wait_ge(*emptied("out", t))
                        dve.sem_inc(out_done, 1)
            turns(dve, body)


_LAID = {
    "wqkv": lambda i: np.concatenate([i["L0_attn_Wq"].T, i["L0_attn_Wk"].T, i["L0_attn_Wv"].T], axis=1),
    "wa": lambda i: i["L0_attn_Wa"].T,
    "wbeta": lambda i: i["L0_attn_Wb"].T,
    "conv_w": lambda i: np.concatenate([i["L0_attn_qcw"], i["L0_attn_kcw"], i["L0_attn_vcw"]])
                          .reshape(MT, 128, TAPS).transpose(1, 0, 2),
    "conv_b": lambda i: np.concatenate([i["L0_attn_qcb"], i["L0_attn_kcb"], i["L0_attn_vcb"]]).reshape(MT, 128).T,
    "wg": lambda i: i["L0_attn_Wg"].T,
    "wsm": lambda i: np.concatenate([i["L0_ffn_gate_W"].T, i["L0_ffn_lora_down"].reshape(ER, HID).T], axis=1),
    "wbase": lambda i: i["L0_ffn_W_base"].T,
    "wo": lambda i: i["L0_attn_Wo"].T,
    "lup": lambda i: np.pad(i["L0_ffn_lora_up"].transpose(0, 2, 1).reshape(ER, HID), ((0, 128 - ER), (0, 0))),
    "wqk": lambda i: i["L1_attn_w_qkv"][:, 0:512].reshape(HID, 2, 2, 128).transpose(0, 2, 1, 3).reshape(HID, 512),
    "bqk": lambda i: i["L1_attn_b_qkv"][0:512].reshape(2, 2, 128).transpose(1, 0, 2).reshape(QK_TILES, 128).T,
    "wv": lambda i: i["L1_attn_w_qkv"][:, 512:768],
    "bv": lambda i: i["L1_attn_b_qkv"][512:768],
    "aT": lambda i: i["L1_ffn_a"].T,
}
_AS_IS = ["L0_attn_x", "L0_attn_ba", "L0_attn_bb", "L0_ffn_gate_b", "L0_ffn_b_base", "L0_attn_ln_w", "L0_attn_ln_b",
          "L1_attn_w_out", "L1_attn_b_out", "L1_ffn_bias", "L1_ffn_kernel", "L1_ffn_b"]


def program(nc, ins, out):
    o_dram = nc.dram_tensor("o_dram", [T, B, H, DV], f32).ap()
    layer0_recurrence(nc, ins, o_dram)
    layer0_end_and_layer1(nc, ins, o_dram, out)


def kernel(**inputs):
    import concourse.bacc as bacc
    from concourse.bass_utils import run_bass_kernel_spmd

    arrays = {name: np.asarray(inputs[name]) for name in inputs}
    arrays = {name: arrays[name] for name in _AS_IS} | {name: lay(arrays) for name, lay in _LAID.items()}
    arrays = {name: np.ascontiguousarray(a) for name, a in arrays.items()}
    nc = bacc.Bacc("TRN2", target_bir_lowering=False, num_devices=1)
    ins = {name: nc.dram_tensor(f"in_{name}", a.shape, f32, kind="ExternalInput").ap() for name, a in arrays.items()}
    out = nc.dram_tensor("out", [B, T, HID], f32, kind="ExternalOutput").ap()
    program(nc, ins, out)
    result = run_bass_kernel_spmd(nc, [{f"in_{name}": a for name, a in arrays.items()}], core_ids=[0])
    return result.results[0]["out"]
```
